# Optimizing a Trainium2 kernel written in Bass

```python
import numpy as np
import jax
import jax.numpy as jnp

def _softmax(x, axis=-1):
    return jax.nn.softmax(x, axis=axis)

def _gelu(x):
    return jax.nn.gelu(x, approximate=True)

def _silu(x):
    return jax.nn.silu(x)

def _sigmoid(x):
    return jax.nn.sigmoid(x)

def _layernorm(x, axis=-1, eps=1e-05):
    m = jnp.mean(x, axis=axis, keepdims=True)
    v = jnp.var(x, axis=axis, keepdims=True)
    return (x - m) / jnp.sqrt(v + eps)

def _scatter_add(tgt, idx, src, axis=0):
    return tgt.at[idx].add(src)

def _segment_sum(src, seg, n):
    return jax.ops.segment_sum(src, seg, n)
kernel_name = 'mk_gnn_preln_d4_gnn_r8_1c03f0'

def setup_inputs(seed: int=0):
    np.random.seed(seed)
    _w = jnp.asarray

    def _rec_inputs():
        import jax
        import jax.numpy as jnp
        _gk = jax.random.key(seed)
        x = -0.000202 + 1 * jax.random.normal(jax.random.fold_in(_gk, 1), (12500, 64), jnp.float32)
        src = jax.random.randint(jax.random.fold_in(_gk, 2), (200000,), 0, 12500, jnp.int32)
        dst = jnp.minimum((12500 * jax.random.uniform(jax.random.fold_in(_gk, 3), (200000,)) ** 2.0).astype(jnp.int32), 99999)
        _o = jnp.argsort(dst, stable=True)
        src = src[_o]
        dst = dst[_o]
        edge_attr_32 = -9.77346e-05 + 0.999888 * jax.random.normal(jax.random.fold_in(_gk, 13), (200000, 32), jnp.float32)
        edge_type_16 = jax.random.randint(jax.random.fold_in(_gk, 15), (200000,), 0, 16, jnp.int32)
        return (x, src, dst, edge_attr_32, edge_type_16)
    x, src, dst, edge_attr_32, edge_type_16 = _rec_inputs()

    def _L0_gnn_setup():
        import jax, jax.numpy as jnp
        import numpy as np
        N_NODES = 12500
        N_EDGES = 125000
        IN_FEAT = 64
        OUT_FEAT = 64
        NUM_RELS = 16
        key = jax.random.key(seed)
        ks = jax.random.split(key, 7)
        xavier = np.sqrt(2.0) * np.sqrt(6.0 / (IN_FEAT + OUT_FEAT))
        feat = jax.random.normal(ks[0], (N_NODES, IN_FEAT), dtype=jnp.float32)
        weight = jax.random.uniform(ks[1], (NUM_RELS, IN_FEAT, OUT_FEAT), dtype=jnp.float32, minval=-xavier, maxval=xavier)
        h_bias = jnp.zeros((OUT_FEAT,), dtype=jnp.float32)
        loop_weight = jax.random.uniform(ks[2], (IN_FEAT, OUT_FEAT), dtype=jnp.float32, minval=-xavier, maxval=xavier)
        src = jax.random.randint(ks[3], (N_EDGES,), 0, N_NODES, dtype=jnp.int32)
        dst = jax.random.randint(ks[4], (N_EDGES,), 0, N_NODES, dtype=jnp.int32)
        etype = jax.random.randint(ks[5], (N_EDGES,), 0, NUM_RELS, dtype=jnp.int32)
        return {'feat': feat, 'weight': weight, 'h_bias': h_bias, 'loop_weight': loop_weight, 'src': src, 'dst': dst, 'etype': etype}
    _L0_gnn_all = _L0_gnn_setup()
    _L0_gnn_in = {k: v for k, v in _L0_gnn_all.items() if k in ('weight', 'h_bias', 'loop_weight')}
    del _L0_gnn_all

    def _L1_gnn_setup():
        import jax, jax.numpy as jnp
        import numpy as np
        N_NODES = 12500
        key = jax.random.key(seed)
        k1, k2, k3, k4, k5 = jax.random.split(key, 5)
        feature = jax.random.normal(k1, (N_NODES, 64), dtype=jnp.float32)
        src = jax.random.randint(k2, (200000,), 0, N_NODES, dtype=jnp.int64)
        dst = jax.random.randint(k3, (200000,), 0, N_NODES, dtype=jnp.int64)
        W = jax.random.normal(k4, (64, 128), dtype=jnp.float32) * 0.05
        b = jax.random.normal(k5, (64,), dtype=jnp.float32) * 0.05
        return {'feature': feature, 'src': src, 'dst': dst, 'W': W, 'b': b}
    _L1_gnn_all = _L1_gnn_setup()
    _L1_gnn_in = {k: v for k, v in _L1_gnn_all.items() if k in ('W', 'b')}
    del _L1_gnn_all

    def _L2_gnn_setup():
        import jax, jax.numpy as jnp
        import numpy as np
        N_NODES = 12500
        N_EDGES = 200000
        NODE_F = 64
        EDGE_F = 32
        OUT_F = 64
        HIDDEN = 2 * OUT_F
        IN_F = 2 * NODE_F + EDGE_F
        key = jax.random.key(seed)
        ks = jax.random.split(key, 8)
        nodes = jax.random.normal(ks[0], (N_NODES, NODE_F), dtype=jnp.float32)
        edges = jax.random.normal(ks[1], (N_EDGES, EDGE_F), dtype=jnp.float32)
        senders = jax.random.randint(ks[2], (N_EDGES,), 0, N_NODES, dtype=jnp.int32)
        receivers = jax.random.randint(ks[3], (N_EDGES,), 0, N_NODES, dtype=jnp.int32)
        W1 = jax.random.normal(ks[4], (IN_F, HIDDEN), dtype=jnp.float32) / np.sqrt(IN_F)
        b1 = jnp.zeros((HIDDEN,), dtype=jnp.float32)
        W2 = jax.random.normal(ks[5], (HIDDEN, OUT_F), dtype=jnp.float32) / np.sqrt(HIDDEN)
        b2 = jnp.zeros((OUT_F,), dtype=jnp.float32)
        Wn = jax.random.normal(ks[6], (NODE_F, OUT_F), dtype=jnp.float32) / np.sqrt(NODE_F)
        bn = jnp.zeros((OUT_F,), dtype=jnp.float32)
        return {'nodes': nodes, 'edges': edges, 'senders': senders, 'receivers': receivers, 'W1': W1, 'b1': b1, 'W2': W2, 'b2': b2, 'Wn': Wn, 'bn': bn}
    _L2_gnn_all = _L2_gnn_setup()
    _L2_gnn_in = {k: v for k, v in _L2_gnn_all.items() if k in ('W1', 'b1', 'W2', 'b2', 'Wn', 'bn')}
    del _L2_gnn_all

    def _L3_gnn_setup():
        import jax, jax.numpy as jnp
        import numpy as np
        N = 12500
        E = 200000
        ENC_EDGE = 32
        ENC_NODE = 64
        HIDDEN = 128
        key = jax.random.key(seed)
        ks = jax.random.split(key, 8)
        x = jax.random.normal(ks[0], (N, ENC_NODE), dtype=jnp.float32)
        edge_index = jax.random.randint(ks[1], (2, E), 0, N, dtype=jnp.int64)
        edge_attr = jax.random.normal(ks[2], (E, ENC_EDGE), dtype=jnp.float32)
        u = jax.random.normal(ks[3], (256, ENC_NODE), dtype=jnp.float32)
        batch = jax.random.randint(ks[4], (N,), 0, 256, dtype=jnp.int64)
        in1 = ENC_EDGE + ENC_NODE
        lim1 = float(np.sqrt(6.0 / (in1 + HIDDEN)))
        W1 = jax.random.uniform(ks[5], (in1, HIDDEN), minval=-lim1, maxval=lim1, dtype=jnp.float32)
        b1 = jnp.full((HIDDEN,), 0.01, dtype=jnp.float32)
        in2 = HIDDEN + ENC_NODE
        lim2 = float(np.sqrt(6.0 / (in2 + ENC_NODE)))
        W2 = jax.random.uniform(ks[6], (in2, ENC_NODE), minval=-lim2, maxval=lim2, dtype=jnp.float32)
        b2 = jnp.full((ENC_NODE,), 0.01, dtype=jnp.float32)
        return {'x': x, 'edge_index': edge_index, 'edge_attr': edge_attr, 'u': u, 'batch': batch, 'W1': W1, 'b1': b1, 'W2': W2, 'b2': b2}
    _L3_gnn_all = _L3_gnn_setup()
    _L3_gnn_in = {k: v for k, v in _L3_gnn_all.items() if k in ('u', 'W1', 'b1', 'W2', 'b2')}
    del _L3_gnn_all
    return {'x': x, 'src': src, 'dst': dst, 'edge_attr_32': edge_attr_32, 'edge_type_16': edge_type_16, 'L0_gnn_weight': _L0_gnn_in['weight'], 'L0_gnn_h_bias': _L0_gnn_in['h_bias'], 'L0_gnn_loop_weight': _L0_gnn_in['loop_weight'], 'L1_gnn_W': _L1_gnn_in['W'], 'L1_gnn_b': _L1_gnn_in['b'], 'L2_gnn_W1': _L2_gnn_in['W1'], 'L2_gnn_b1': _L2_gnn_in['b1'], 'L2_gnn_W2': _L2_gnn_in['W2'], 'L2_gnn_b2': _L2_gnn_in['b2'], 'L2_gnn_Wn': _L2_gnn_in['Wn'], 'L2_gnn_bn': _L2_gnn_in['bn'], 'L3_gnn_u': _L3_gnn_in['u'], 'L3_gnn_W1': _L3_gnn_in['W1'], 'L3_gnn_b1': _L3_gnn_in['b1'], 'L3_gnn_W2': _L3_gnn_in['W2'], 'L3_gnn_b2': _L3_gnn_in['b2']}

def reference(x, src, dst, edge_attr_32, edge_type_16, L0_gnn_weight, L0_gnn_h_bias, L0_gnn_loop_weight, L1_gnn_W, L1_gnn_b, L2_gnn_W1, L2_gnn_b1, L2_gnn_W2, L2_gnn_b2, L2_gnn_Wn, L2_gnn_bn, L3_gnn_u, L3_gnn_W1, L3_gnn_b1, L3_gnn_W2, L3_gnn_b2):
    import jax
    import jax.numpy as jnp

    def _L0_gnn_ref(feat, weight, h_bias, loop_weight, src, dst, etype):
        import jax, jax.numpy as jnp
        import numpy as np
        N_NODES = 12500
        N_EDGES = 125000
        IN_FEAT = 64
        OUT_FEAT = 64
        NUM_RELS = 16
        xproj = jnp.einsum('ni,rio->rno', feat, weight)
        m = xproj[etype, src]
        agg = jax.ops.segment_sum(m, dst, num_segments=feat.shape[0])
        return agg + h_bias + feat @ loop_weight

    def _L1_gnn_ref(feature, src, dst, W, b):
        import jax, jax.numpy as jnp
        import numpy as np
        N_NODES = 12500
        agg = jax.ops.segment_sum(feature[src], dst, num_segments=feature.shape[0])
        h = jnp.concatenate([feature, agg], axis=1)
        return h @ W.T + b

    def _L2_gnn_ref(nodes, edges, senders, receivers, W1, b1, W2, b2, Wn, bn):
        import jax, jax.numpy as jnp
        import numpy as np
        N_NODES = 12500
        N_EDGES = 200000
        NODE_F = 64
        EDGE_F = 32
        OUT_F = 64
        HIDDEN = 2 * OUT_F
        IN_F = 2 * NODE_F + EDGE_F
        n_nodes = nodes.shape[0]
        sender_features = nodes[senders]
        receiver_features = nodes[receivers]
        concat = jnp.concatenate([sender_features, receiver_features, edges], axis=-1)
        h = jax.nn.relu(concat @ W1 + b1)
        messages = h @ W2 + b2
        aggregated = jax.ops.segment_sum(messages, receivers, num_segments=n_nodes)
        degree = jax.ops.segment_sum(jnp.ones((receivers.shape[0],), dtype=messages.dtype), receivers, num_segments=n_nodes)
        aggregated = aggregated / jnp.maximum(degree, 1.0)[:, None]
        new_nodes = aggregated + (nodes @ Wn + bn)
        return new_nodes

    def _L3_gnn_ref(x, edge_index, edge_attr, u, batch, W1, b1, W2, b2):
        import jax, jax.numpy as jnp
        import numpy as np
        N = 12500
        E = 200000
        ENC_EDGE = 32
        ENC_NODE = 64
        HIDDEN = 128
        row, col = (edge_index[0], edge_index[1])
        msg = jnp.concatenate([x[row], edge_attr], axis=1)
        msg = msg @ W1 + b1
        agg = jax.ops.segment_sum(msg, col, num_segments=x.shape[0])
        out = jnp.concatenate([x, agg], axis=1)
        return out @ W2 + b2
    edge_index = jnp.stack([src, dst])
    batch0 = jnp.zeros((12500,), jnp.int32)
    h = jnp.maximum(_layernorm(x, axis=-1), 0.0)
    x = x + _L0_gnn_ref(h, L0_gnn_weight, L0_gnn_h_bias, L0_gnn_loop_weight, src, dst, edge_type_16)
    h = jnp.maximum(_layernorm(x, axis=-1), 0.0)
    x = x + _L1_gnn_ref(h, src, dst, L1_gnn_W, L1_gnn_b)
    h = jnp.maximum(_layernorm(x, axis=-1), 0.0)
    x = x + _L2_gnn_ref(h, edge_attr_32, src, dst, L2_gnn_W1, L2_gnn_b1, L2_gnn_W2, L2_gnn_b2, L2_gnn_Wn, L2_gnn_bn)
    h = jnp.maximum(_layernorm(x, axis=-1), 0.0)
    x = x + _L3_gnn_ref(h, edge_index, edge_attr_32, L3_gnn_u, batch0, L3_gnn_W1, L3_gnn_b1, L3_gnn_W2, L3_gnn_b2)
    return x

_drawn_inputs = setup_inputs


def setup_inputs(seed=0):
    import zlib

    import numpy as np

    out = dict(_drawn_inputs(seed))
    spreads = {'L0_gnn_h_bias': (0.0, 0.1),
     'L2_gnn_b1': (0.0, 0.567),
     'L2_gnn_b2': (0.0, 0.316),
     'L2_gnn_bn': (0.0, 0.292),
     'L3_gnn_b1': (0.009999999776482582, 0.6),
     'L3_gnn_b2': (0.009999999776482582, 0.6)}
    factors = {'L1_gnn_b': 4.8}
    for name, (base, spread) in spreads.items():
        noise = np.random.default_rng([zlib.crc32(name.encode()), seed]).standard_normal(out[name].shape)
        drawn = base * np.exp(spread * noise) if base else spread * noise
        out[name] = jnp.asarray(drawn.astype(out[name].dtype))
    for name, factor in factors.items():
        out[name] = (out[name] * factor).astype(out[name].dtype)
    return out
```

```python
from contextlib import ExitStack

import concourse.bass as bass
from concourse import mybir

F32 = mybir.dt.float32
BF16 = mybir.dt.bfloat16
I32 = mybir.dt.int32
ALU = mybir.AluOpType
ACT = mybir.ActivationFunctionType
AX = mybir.AxisListType
DVE_ENGINE = mybir.EngineType.DVE
SP_ENGINE = mybir.EngineType.SP

P = 128
D = 64
FE = 32
H = 128
RELS = 16
N = 12500
E = 200000

KW = 7
BLK = P * KW
NB = -(-N // BLK)
NPAD = NB * BLK
ACC_W = NPAD + P
PAIRS = NB // 2

TILES = 4
GE = P * TILES
SLOTS = 4
ITERS = -(-E // (GE * SLOTS))
G = ITERS * SLOTS
CH = -(-G // P)
PAD_DST = -1000000.0
MAX_PASSES = -(-N // P)
EPS = 1e-5

assert NB % 2 == 0 and GE == 512


def gnn_program(nc, x, src, dst, edge_attr, edge_type, w_rel, b_rel, w_loop, w_sum, b_sum,
                w1_mlp, b1_mlp, w2_mlp, b2_mlp, wn_mlp, bn_mlp, w1_lin, b1_lin, w2_lin, b2_lin, out):
    rel_table = nc.dram_tensor("rel_table", [NPAD * RELS, D], F32).ap()
    h1_table = nc.dram_tensor("h1_table", [NPAD, D], F32).ap()
    snd_table = nc.dram_tensor("snd_table", [NPAD, H], F32).ap()
    rcv_table = nc.dram_tensor("rcv_table", [ACC_W, H], F32).ap()
    h3_table = nc.dram_tensor("h3_table", [NPAD, D], F32).ap()

    with ExitStack() as ctx:
        def sb(name, shape, dt=F32, scope=ctx):
            return scope.enter_context(nc.sbuf_tensor(name, shape, dt))

        held = []

        def sem(name):
            held.append(nc.alloc_semaphore(name=name))
            return held[-1]

        def end_phase():
            nc.clear_and_free_semaphores(held)
            held.clear()
            nc.all_engine_barrier()

        xs = sb("xs", [P, NB, KW * D])
        acc = sb("acc", [P, ACC_W])
        rel_dst = sb("rel_dst", [P, G * TILES])
        idx_src = sb("idx_src", [P, G * TILES], I32)
        idx_rel = sb("idx_rel", [P, G * TILES], I32)
        base_row = sb("base_row", [1, CH * P], I32)
        passes = sb("passes", [1, 1], I32)
        iota = sb("iota", [P, P])
        window_iota = sb("window_iota", [P, P])
        ident = sb("ident", [P, P])
        ident_bf = sb("ident_bf", [P, P], BF16)
        wc0 = sb("wc0", [D + 1, D + RELS * D])
        wc1 = sb("wc1", [D + 1, D])
        wc2 = sb("wc2", [D + 1, D + 2 * H])
        wc3 = sb("wc3", [D + 1, D])
        wp1 = sb("wp1", [D, D])
        wp2 = sb("wp2", [H, D + 1])
        wp2_deg = sb("wp2_deg", [D + FE + 1, D + 1])
        wp3a = sb("wp3a", [D + FE + 1, H])
        wp3b = sb("wp3b", [H, D])
        w_edge = sb("w_edge", [P, TILES * H])

        setup(nc, sem, locals())
        end_phase()
        hidden_acc = sb("hidden_acc", [P, ACC_W])

        wc = [wc0, wc1, wc2, wc3]
        tables = [rel_table, h1_table, (snd_table, rcv_table), h3_table]
        post = [(acc, ident), (acc, wp1), (hidden_acc, wp2), (acc, wp3a)]
        for layer in range(4):
            node_phase(nc, sem, layer, xs, acc, post[layer - 1] if layer else None, wp2_deg, wp3b,
                       wc[layer], tables[layer], ident, None)
            end_phase()
            edge_phase(nc, sem, layer, acc if layer != 2 else hidden_acc, tables[layer],
                       idx_rel if layer == 0 else idx_src, rel_dst, base_row, passes, iota, window_iota,
                       ident, ident_bf, w_edge, edge_attr)
            end_phase()
        node_phase(nc, sem, 4, xs, acc, post[3], wp2_deg, wp3b, None, None, ident, out)


def setup(nc, sem, env):
    x, src, dst, edge_type = env["x"], env["src"], env["dst"], env["edge_type"]
    xs, ident, iota, ident_bf = env["xs"], env["ident"], env["iota"], env["ident_bf"]
    wc0, wc1, wc2, wc3 = env["wc0"], env["wc1"], env["wc2"], env["wc3"]
    wp1, wp2, wp2_deg, wp3a, wp3b = env["wp1"], env["wp2"], env["wp2_deg"], env["wp3a"], env["wp3b"]
    w_edge, acc, base_row, passes = env["w_edge"], env["acc"], env["base_row"], env["passes"]

    zeroed = sem("setup_zeroed")
    const_ready = sem("setup_const_ready")
    loaded = sem("setup_loaded")
    chain = sem("setup_chain")
    bad_ready = sem("setup_bad_ready")
    bad_summed = sem("setup_bad_summed")
    lists_ready = sem("setup_lists_ready")
    turned = sem("setup_turned")
    evacuated = sem("setup_evacuated")

    with ExitStack() as scope:
        def sb(name, shape, dt=F32):
            return scope.enter_context(nc.sbuf_tensor(name, shape, dt))

        raw_dst = sb("raw_dst", [P, CH, GE], I32)
        raw_src = sb("raw_src", [P, CH, GE], I32)
        raw_typ = sb("raw_typ", [P, CH, GE], I32)
        dst_f = sb("dst_f", [P, CH, GE])
        src_f = sb("src_f", [P, CH, GE])
        row_f = sb("row_f", [P, CH, GE])
        off_f = sb("off_f", [P, CH, GE])
        real = sb("real", [P, CH, GE])
        bad = sb("bad", [P, CH, GE])
        first = sb("first", [P, CH])
        base_f = sb("base_f", [P, CH])
        any_bad = sb("any_bad", [P, 1])
        fast = sb("fast", [P, 1])
        ones = sb("ones", [P, P])
        part = sb("part", [P, 1])
        w_sum_raw = sb("w_sum_raw", [D, 2 * D])
        turn_ps = [scope.enter_context(nc.psum_tensor(f"turn_ps{i}", [P, 512], F32)) for i in range(4)]
        row_ps = scope.enter_context(nc.psum_tensor("row_ps", [P, 512], F32))
        sum_ps = scope.enter_context(nc.psum_tensor("sum_ps", [P, 512], F32))
        w_ps = scope.enter_context(nc.psum_tensor("w_ps", [P, 512], F32))

        full_rows = E // (P * GE) * P * GE
        tail_rows = (E - full_rows) // GE
        tail_edges = E - full_rows - tail_rows * GE
        full_blocks = N // BLK
        tail_parts = (N - full_blocks * BLK) // KW
        tail_nodes = N - full_blocks * BLK - tail_parts * KW
        lists = [(env["rel_dst"], off_f), (env["idx_src"], src_f), (env["idx_rel"], row_f)]

        with nc.Block() as block:
            @block.gpsimd
            def _(pool):
                nc.gpsimd.memset(raw_dst[:, CH - 1, :], int(PAD_DST)).then_inc(zeroed, 1)
                nc.gpsimd.memset(raw_src[:, CH - 1, :], 0).then_inc(zeroed, 1)
                nc.gpsimd.memset(raw_typ[:, CH - 1, :], 0).then_inc(zeroed, 1)
                nc.gpsimd.memset(xs[:, NB - 1, :], 0.0).then_inc(zeroed, 1)
                nc.gpsimd.memset(w_edge[:, :], 0.0).then_inc(zeroed, 1)
                nc.gpsimd.memset(wc0[:, :], 0.0).then_inc(zeroed, 1)
                nc.gpsimd.memset(wc2[:, :], 0.0).then_inc(zeroed, 1)
                nc.gpsimd.memset(wp2[:, :], 0.0).then_inc(zeroed, 1)
                nc.gpsimd.memset(wp2_deg[:, :], 1.0).then_inc(zeroed, 1)
                nc.gpsimd.iota(iota[:, :], [[1, P]], base=0, channel_multiplier=0,
                               allow_small_or_imprecise_dtypes=True).then_inc(const_ready, 1)
                nc.gpsimd.iota(part[:, :], [[0, 1]], base=0, channel_multiplier=1,
                               allow_small_or_imprecise_dtypes=True).then_inc(const_ready, 1)
                nc.gpsimd.memset(ones[:, :], 1.0).then_inc(const_ready, 1)

            @block.sync
            def _(sp):
                loads = []
                sp.wait_ge(zeroed, 9)
                for raw, edges in ((raw_dst, dst), (raw_src, src), (raw_typ, edge_type)):
                    loads.append((raw[:, 0:CH - 1, :],
                                  edges[0:full_rows].rearrange("(c g e) -> g c e", g=P, e=GE)))
                    loads.append((raw[0:tail_rows, CH - 1, :],
                                  edges[full_rows:full_rows + tail_rows * GE].rearrange("(g e) -> g e", e=GE)))
                    loads.append((raw[tail_rows:tail_rows + 1, CH - 1, 0:tail_edges],
                                  edges[E - tail_edges:E].rearrange("(a e) -> a e", a=1)))
                n0 = full_blocks * BLK
                loads.append((xs[:, 0:full_blocks, :],
                              x[0:n0, :].rearrange("(b p k) f -> p b (k f)", p=P, k=KW)))
                loads.append((xs[0:tail_parts, full_blocks, :],
                              x[n0:n0 + tail_parts * KW, :].rearrange("(p k) f -> p (k f)", k=KW)))
                loads.append((xs[tail_parts:tail_parts + 1, full_blocks, 0:tail_nodes * D],
                              x[N - tail_nodes:N, :].rearrange("(a k) f -> a (k f)", a=1)))
                bias = lambda b: b.rearrange("(a f) -> a f", a=1)
                loads.append((wc0[0:D, 0:D], env["w_loop"]))
                loads.append((wc0[0:D, D:].rearrange("i (r o) -> i r o", r=RELS),
                              env["w_rel"].rearrange("r i o -> i r o")))
                loads.append((wc0[D:D + 1, 0:D], bias(env["b_rel"])))
                loads.append((w_sum_raw[:, :], env["w_sum"]))
                loads.append((wc1[D:D + 1, :], bias(env["b_sum"])))
                loads.append((wc2[0:D, 0:D], env["wn_mlp"]))
                loads.append((wc2[0:D, D:D + H], env["w1_mlp"][0:D, :]))
                loads.append((wc2[0:D, D + H:], env["w1_mlp"][D:2 * D, :]))
                loads.append((wc2[D:D + 1, 0:D], bias(env["bn_mlp"])))
                loads.append((wc2[D:D + 1, D + H:], bias(env["b1_mlp"])))
                for u in range(TILES):
                    loads.append((w_edge[FE * u:FE * u + FE, H * u:H * u + H], env["w1_mlp"][2 * D:, :]))
                loads.append((wp2[:, 0:D], env["w2_mlp"]))
                loads.append((wp2_deg[D + FE:D + FE + 1, 0:D], bias(env["b2_mlp"])))
                loads.append((wc3[0:D, :], env["w2_lin"][0:D, :]))
                loads.append((wc3[D:D + 1, :], bias(env["b2_lin"])))
                loads.append((wp3a[0:D + FE, :], env["w1_lin"]))
                loads.append((wp3a[D + FE:D + FE + 1, :], bias(env["b1_lin"])))
                loads.append((wp3b[:, :], env["w2_lin"][D:, :]))
                for to, of in loads:
                    sp.dma_start(to, of).then_inc(loaded, 16)
                sp.wait_ge(loaded, 16 * len(loads))
                sp.sem_inc(loaded, 1)

            n_loads = 9 + 3 + 10 + TILES + 7
            all_loaded = 16 * n_loads + 1

            @block.vector
            def _(dve):
                done = [0]

                def link(ins):
                    done[0] += 1
                    ins.then_inc(chain, 1)
                    dve.wait_ge(chain, done[0])

                dve.wait_ge(const_ready, 3)
                link(nc.vector.tensor_scalar(ident[:, :], iota[:, :], part[:, 0:1], None, ALU.is_equal))
                link(nc.vector.tensor_copy(ident_bf[:, :], ident[:, :]))
                dve.wait_ge(loaded, all_loaded)
                nc.vector.tensor_copy(src_f[:, :, :], raw_src[:, :, :])
                nc.vector.tensor_copy(dst_f[:, :, :], raw_dst[:, :, :])
                link(nc.vector.tensor_copy(row_f[:, :, :], raw_typ[:, :, :]))
                link(nc.vector.scalar_tensor_tensor(out=row_f[:, :, :], in0=src_f[:, :, :],
                                                    scalar=float(RELS), in1=row_f[:, :, :],
                                                    op0=ALU.mult, op1=ALU.add))
                link(nc.vector.tensor_scalar(first[:, :], dst_f[:, :, 0], 0.0, None, ALU.max))

                def spread(t):
                    return t[:, :].unsqueeze(2).to_broadcast([P, CH, GE])

                nc.vector.tensor_scalar(real[:, :, :], dst_f[:, :, :], 0.0, None, ALU.is_ge)
                link(nc.vector.tensor_tensor(off_f[:, :, :], dst_f[:, :, :], spread(first), ALU.subtract))
                link(nc.vector.scalar_tensor_tensor(out=real[:, :, :], in0=off_f[:, :, :], scalar=0.0,
                                                    in1=real[:, :, :], op0=ALU.is_lt, op1=ALU.mult))
                link(nc.vector.scalar_tensor_tensor(out=bad[:, :, :], in0=off_f[:, :, :], scalar=float(P),
                                                    in1=real[:, :, :], op0=ALU.is_ge, op1=ALU.add))
                nc.vector.tensor_reduce(any_bad[:, :], bad[:, :, :], AX.XY, ALU.max).then_inc(bad_ready, 1)
                dve.wait_ge(bad_summed, 1)
                link(nc.vector.tensor_scalar(fast[:, :], sum_ps[:, 0:1], 0.0, None, ALU.is_equal))
                nc.vector.tensor_scalar(passes[:, :], fast[0:1, :], float(1 - MAX_PASSES), float(MAX_PASSES),
                                        ALU.mult, ALU.add)
                link(nc.vector.tensor_scalar(base_f[:, :], first[:, :], fast[:, 0:1], None, ALU.mult))
                nc.vector.tensor_tensor(off_f[:, :, :], dst_f[:, :, :], spread(base_f),
                                        ALU.subtract).then_inc(lists_ready, 1)
                dve.wait_ge(turned, len(lists) * CH + 1)
                nc.vector.tensor_copy(base_row[:, :], row_ps[0:1, 0:CH * P])
                dve.wait_ge(turned, len(lists) * CH + 3)
                nc.vector.tensor_copy(wc1[0:D, :], w_ps[0:D, 0:D])
                nc.vector.tensor_copy(wp1[:, :], w_ps[0:D, D:2 * D])

            @block.tensor
            def _(pe):
                pe.wait_ge(bad_ready, 1)
                nc.tensor.matmul(sum_ps[:, 0:1], ones[:, :], any_bad[:, :], start=True,
                                 stop=True).then_inc(bad_summed, 1)
                pe.wait_ge(lists_ready, 1)
                for a, (_, laid) in enumerate(lists):
                    for c in range(CH):
                        n = a * CH + c
                        if n >= 4:
                            pe.wait_ge(evacuated, n - 3)
                        view = laid[:, c, :].rearrange("g (p u) -> g u p", u=TILES)
                        for u in range(TILES):
                            last = nc.tensor.transpose(turn_ps[n % 4][:, u * P:(u + 1) * P], view[:, u, :],
                                                       ident[:, :])
                        last.then_inc(turned, 1)
                for c in range(CH):
                    last = nc.tensor.matmul(row_ps[0:1, c * P:(c + 1) * P], base_f[:, c:c + 1], ident[:, :],
                                            start=True, stop=True)
                last.then_inc(turned, 1)
                for half in range(2):
                    nc.tensor.transpose(w_ps[0:D, half * D:(half + 1) * D],
                                        w_sum_raw[:, half * D:(half + 1) * D],
                                        ident[0:D, 0:D]).then_inc(turned, 1)

            @block.scalar
            def _(act):
                for n in range(len(lists) * CH):
                    to, c = lists[n // CH][0], n % CH
                    groups = min(P, G - c * P)
                    act.wait_ge(turned, n + 1)
                    nc.scalar.copy(
                        to[:, c * GE:c * GE + groups * TILES].rearrange("p (g u) -> p u g", u=TILES),
                        turn_ps[n % 4][:, :].rearrange("p (u g) -> p u g", u=TILES)[:, :, 0:groups],
                    ).then_inc(evacuated, 1)


def node_phase(nc, sem, layer, xs, acc, post, wp2_deg, wp3b, wc, table, ident, out):
    name = f"node{layer}_"
    after = layer - 1
    last_phase = layer == 4
    staged = sem(name + "staged")
    post_ready = sem(name + "post_ready")
    x_posted = sem(name + "x_posted")
    lin_ready = sem(name + "lin_ready")
    lin_copied = sem(name + "lin_copied")
    step = sem(name + "step")
    var_ready = sem(name + "var_ready")
    std_ready = sem(name + "std_ready")
    h_ready = sem(name + "h_ready")
    turn_begun = sem(name + "turn_begun")
    turned = sem(name + "turned")
    ht_ready = sem(name + "ht_ready")
    own_ready = sem(name + "own_ready")
    own_added = sem(name + "own_added")
    rows_ready = sem(name + "rows_ready")
    rows_copied = sem(name + "rows_copied")
    stored = [sem(name + f"stored{i}") for i in range(2)]

    with ExitStack() as scope:
        def sb(n, shape, dt=F32):
            return scope.enter_context(nc.sbuf_tensor(name + n, shape, dt))

        def ps(n, shape):
            return scope.enter_context(nc.psum_tensor(name + n, shape, F32))

        small = sb("small", [P, 4, KW])
        xc = sb("xc", [P, KW, D])
        sq = sb("sq", [P, KW, D])
        h = [sb(f"h{i}", [P, KW, D]) for i in range(2)]
        ht = [sb(f"ht{i}", [D + 1, KW * P]) for i in range(2)]
        lin = sb("lin", [P, BLK])
        stage = [sb(f"stage{i}", [P, BLK]) for i in range(2)] if after >= 0 else None
        stage_deg = [sb(f"stage_deg{i}", [P, BLK]) for i in range(2)] if after == 2 else None
        rows = [sb(f"rows{i}", [P, RELS * D] if layer == 0 else [P, 2, KW * H]) for i in range(2)] \
            if layer in (0, 2) else None
        zero_rows = sb("zero_rows", [P, H]) if layer == 2 else None
        zero_ready = sem(name + "zero_ready")
        post_ps = ps("post_ps", [P, 512])
        own_ps = ps("own_ps", [P, 512])
        ht_ps = ps("ht_ps", [P, 1024])
        row_ps = [ps(f"row_ps{i}", [P, 1024]) for i in range(2)]
        width = D + 1 if after == 2 else D
        stores = KW if layer == 0 else 2 if layer == 2 else 1
        steps = (0 if after < 0 else 4 if after == 2 else 1) + (0 if last_phase else 7)

        with nc.Block() as block:
            @block.gpsimd
            def _(pool):
                if after < 0:
                    return
                k_rows = {0: D, 1: D, 2: H, 3: D + FE + 1}[after]
                with pool.Fori(0, PAIRS) as q:
                    for s in range(2):
                        b = q * 2 + s
                        pool.wait_ge(post_ready, b + 1)
                        nc.gpsimd.tensor_copy(stage[s][0:k_rows, :],
                                              post[0][0:k_rows, bass.ds(b * BLK, BLK)]).then_inc(staged, 1)
                        if after == 2:
                            pool.wait_ge(staged, b * 2 + 1)
                            nc.gpsimd.tensor_copy(stage_deg[s][D + FE:D + FE + 1, :],
                                                  acc[D + FE:D + FE + 1, bass.ds(b * BLK, BLK)]
                                                  ).then_inc(staged, 1)
                            pool.wait_ge(staged, b * 2 + 2)

            @block.tensor
            def _(pe):
                if after >= 0:
                    pe.sem_inc(post_ready, 2)

                def apply_sums(b, s):
                    sums, weights = stage[s], post[1]
                    pe.wait_ge(x_posted, b + 1)
                    pe.wait_ge(staged, (b + 1) * (2 if after == 2 else 1))
                    if after == 3:
                        for half in range(2):
                            cols = BLK // 2
                            last = nc.tensor.matmul(
                                row_ps[half][:, 0:cols], weights[0:D + FE + 1, :],
                                sums[0:D + FE + 1, half * cols:(half + 1) * cols], start=True, stop=True)
                        last.then_inc(lin_ready, 1)
                        pe.wait_ge(lin_copied, b + 1)
                        sums, weights, k_rows = lin, wp3b, H
                    else:
                        k_rows = H if after == 2 else D
                    for k in range(KW):
                        to = post_ps[:, k * width:(k + 1) * width]
                        nodes = slice(k, BLK, KW)
                        last = nc.tensor.matmul(to, sums[0:k_rows, nodes], weights[0:k_rows, 0:width],
                                                start=True, stop=after != 2)
                        if after == 2:
                            last = nc.tensor.matmul(to, stage_deg[s][D + FE:D + FE + 1, nodes],
                                                    wp2_deg[D + FE:D + FE + 1, :], start=False, stop=True)
                    last.then_inc(post_ready, 1)

                def turn_and_project(q, s):
                    b = q * 2 + s
                    pe.wait_ge(h_ready, b + 1)
                    pe.wait_ge(ht_ready, b + 1)
                    pe.sem_inc(turn_begun, 1)
                    for k in range(KW):
                        last = nc.tensor.transpose(ht_ps[0:D, k * P:(k + 1) * P], h[s][:, k, :], ident[:, :])
                    last.then_inc(turned, 1)
                    pe.wait_ge(ht_ready, b + 2)
                    pe.wait_ge(own_added, b + 1)
                    for k in range(KW):
                        last = nc.tensor.matmul(own_ps[:, k * D:(k + 1) * D], ht[s][:, k * P:(k + 1) * P],
                                                wc[:, 0:D], start=True, stop=True)
                    last.then_inc(own_ready, 1)
                    if rows is None:
                        return
                    for k in range(KW):
                        slot = (s * KW + k) % 2
                        pe.wait_ge(rows_copied, b * KW + k + 1)
                        for c in range(0, RELS * D if layer == 0 else 2 * H, 512):
                            cols = min(512, wc.shape[1] - D - c)
                            last = nc.tensor.matmul(row_ps[slot][:, c:c + cols], ht[s][:, k * P:(k + 1) * P],
                                                    wc[:, D + c:D + c + cols], start=True, stop=True)
                        last.then_inc(rows_ready, 1)

                if last_phase:
                    with pe.Fori(0, PAIRS) as q:
                        for s in range(2):
                            apply_sums(q * 2 + s, s)
                elif after < 0:
                    with pe.Fori(0, PAIRS) as q:
                        for s in range(2):
                            turn_and_project(q, s)
                else:
                    apply_sums(0, 0)
                    with pe.Fori(0, PAIRS - 1) as q:
                        for s in range(2):
                            apply_sums(q * 2 + s + 1, 1 - s)
                            turn_and_project(q, s)
                    apply_sums(NB - 1, 1)
                    for s in range(2):
                        turn_and_project(PAIRS - 1, s)

            @block.scalar
            def _(act):
                if not last_phase:
                    act.sem_inc(ht_ready, 1)
                    if rows is not None:
                        act.sem_inc(rows_copied, 2)

                def root(b):
                    act.wait_ge(var_ready, b + 1)
                    nc.scalar.activation(small[:, 2, :], small[:, 2, :], ACT.Sqrt).then_inc(std_ready, 1)

                def copy_out(q, s):
                    b = q * 2 + s
                    act.wait_ge(turned, b + 3)
                    act.wait_ge(own_ready, b + 1)
                    nc.scalar.copy(ht[s][0:D, :], ht_ps[0:D, 0:KW * P]).then_inc(ht_ready, 1)
                    if rows is None:
                        return
                    for k in range(KW):
                        slot = (s * KW + k) % 2
                        act.wait_ge(rows_ready, b * KW + k + 1)
                        if layer == 0:
                            act.wait_ge(stored[slot], 16 * (q * KW + (s * KW + k) // 2 + 1))
                            nc.scalar.copy(rows[slot][:, :], row_ps[slot][:, :]).then_inc(rows_copied, 1)
                        else:
                            if k == 0:
                                act.wait_ge(stored[s], 32 * (q + 1))
                            nc.scalar.copy(
                                rows[s][:, :, k * H:(k + 1) * H],
                                row_ps[slot][:, 0:2 * H].rearrange("p (t f) -> p t f", t=2),
                            ).then_inc(rows_copied, 1)

                if last_phase:
                    with act.Fori(0, NB) as b:
                        act.wait_ge(lin_ready, b + 1)
                        for half in range(2):
                            cols = BLK // 2
                            ins = nc.scalar.copy(lin[:, half * cols:(half + 1) * cols],
                                                 row_ps[half][:, 0:cols])
                        ins.then_inc(lin_copied, 1)
                else:
                    with act.Fori(0, PAIRS) as q:
                        for s in range(2):
                            root(q * 2 + s)
                            copy_out(q, s)

            @block.vector
            def _(dve):
                if not last_phase:
                    for s in range(2):
                        nc.vector.memset(ht[s][D:D + 1, :], 1.0)
                    dve.sem_inc(own_added, 1)
                if zero_rows is not None:
                    nc.vector.memset(zero_rows[:, :], 0.0).then_inc(zero_ready, 1)
                if after >= 0:
                    dve.sem_inc(x_posted, 1)

                def normalise(q, s):
                    b = q * 2 + s
                    xb = xs[:, bass.ds(b, 1), :].rearrange("p a (k f) -> p (a k) f", k=KW)
                    done = [0]

                    def link(ins):
                        done[0] += 1
                        ins.then_inc(step, 1)
                        dve.wait_ge(step, b * steps + done[0])

                    if after >= 0:
                        dve.wait_ge(post_ready, b + 3)
                        add = post_ps[:, 0:KW * width].rearrange("p (k f) -> p k f", f=width)
                        if after == 2:
                            deg = small[:, 0, :].unsqueeze(2)
                            link(nc.vector.tensor_scalar(deg, add[:, :, D:D + 1], 1.0, None, ALU.max))
                            link(nc.vector.reciprocal(deg, deg))
                            link(nc.vector.tensor_tensor(sq[:, :, :], add[:, :, 0:D],
                                                         deg.to_broadcast([P, KW, D]), ALU.mult))
                            add = sq[:, :, :]
                        link(nc.vector.tensor_tensor(xb, xb, add[:, :, 0:D], ALU.add))
                        dve.sem_inc(x_posted, 1)
                    if last_phase:
                        return
                    mean, rstd = small[:, 1, :], small[:, 2, :]
                    link(nc.vector.tensor_reduce(mean, xb, AX.X, ALU.add))
                    link(nc.vector.tensor_scalar(mean, mean, 1.0 / D, None, ALU.mult))
                    link(nc.vector.tensor_tensor(xc[:, :, :], xb, mean.unsqueeze(2).to_broadcast([P, KW, D]),
                                                 ALU.subtract))
                    link(nc.vector.tensor_tensor(sq[:, :, :], xc[:, :, :], xc[:, :, :], ALU.mult))
                    link(nc.vector.tensor_reduce(rstd, sq[:, :, :], AX.X, ALU.add))
                    link(nc.vector.tensor_scalar(rstd, rstd, 1.0 / D, EPS, ALU.mult, ALU.add))
                    dve.sem_inc(var_ready, 1)
                    dve.wait_ge(std_ready, b + 1)
                    link(nc.vector.reciprocal(rstd, rstd))
                    dve.wait_ge(turned, b + 1)
                    if rows is None:
                        dve.wait_ge(stored[s], 16 * (q + 1))
                    nc.vector.scalar_tensor_tensor(out=h[s][:, :, :], in0=xc[:, :, :], scalar=0.0,
                                                   in1=rstd.unsqueeze(2).to_broadcast([P, KW, D]),
                                                   op0=ALU.max, op1=ALU.mult).then_inc(h_ready, 1)

                def add_own(b):
                    xb = xs[:, bass.ds(b, 1), :].rearrange("p a f -> p (a f)")
                    dve.wait_ge(own_ready, b + 2)
                    nc.vector.tensor_tensor(xb, xb, own_ps[:, 0:KW * D], ALU.add).then_inc(own_added, 1)

                if last_phase:
                    with dve.Fori(0, PAIRS) as q:
                        for s in range(2):
                            normalise(q, s)
                else:
                    dve.sem_inc(turned, 2)
                    dve.sem_inc(own_ready, 1)
                    normalise(0, 0)
                    normalise(0, 1)
                    add_own(0)
                    with dve.Fori(1, PAIRS) as q:
                        for s in range(2):
                            normalise(q, s)
                            add_own(q * 2 + s - 1)
                    add_own(NB - 1)

            @block.sync
            def _(sp):
                if last_phase:
                    return
                for s in range(2):
                    sp.sem_inc(stored[s], 16 * (2 if layer == 2 else 1))
                with sp.Fori(0, PAIRS) as q:
                    for s in range(2):
                        b = q * 2 + s
                        if layer == 0:
                            to = table.rearrange("(b p k r) f -> b k p (r f)", p=P, k=KW, r=RELS)
                            for k in range(KW):
                                sp.wait_ge(rows_copied, b * KW + k + 3)
                                slot = (s * KW + k) % 2
                                sp.dma_start(to[bass.ds(b, 1), k].rearrange("a p f -> (a p) f"),
                                             rows[slot][:, :]).then_inc(stored[slot], 16)
                        elif layer == 2:
                            sp.wait_ge(rows_copied, (b + 1) * KW + 2)
                            for t in range(2):
                                to = table[t][0:NPAD, :].rearrange("(b p k) f -> b p (k f)", p=P, k=KW)
                                sp.dma_start(to[bass.ds(b, 1)].rearrange("a p f -> (a p) f"),
                                             rows[s][:, t, :]).then_inc(stored[s], 16)
                        else:
                            sp.wait_ge(h_ready, b + 1)
                            to = table.rearrange("(b p k) f -> b p (k f)", p=P, k=KW)
                            sp.dma_start(to[bass.ds(b, 1)].rearrange("a p f -> (a p) f"),
                                         h[s][:, :, :].rearrange("p k f -> p (k f)")).then_inc(stored[s], 16)
                if layer == 2:
                    sp.wait_ge(zero_ready, 1)
                    sp.dma_start(table[1][NPAD:ACC_W, :], zero_rows[:, :]).then_inc(zero_ready, 16)
                    sp.wait_ge(zero_ready, 17)
                per_slot = KW * PAIRS if layer == 0 else 2 * PAIRS if layer == 2 else PAIRS
                for s in range(2):
                    sp.wait_ge(stored[s], 16 * per_slot + 16 * (2 if layer == 2 else 1))

    if last_phase:
        finished = sem(name + "finished")
        full_blocks = N // BLK
        n0 = full_blocks * BLK
        tail_parts = (N - n0) // KW
        tail_nodes = N - n0 - tail_parts * KW
        with nc.Block() as block:
            @block.sync
            def _(sp):
                sp.dma_start(out[0:n0, :].rearrange("(b p k) f -> p b (k f)", p=P, k=KW),
                             xs[:, 0:full_blocks, :]).then_inc(finished, 16)
                sp.dma_start(out[n0:n0 + tail_parts * KW, :].rearrange("(p k) f -> p (k f)", k=KW),
                             xs[0:tail_parts, full_blocks, :]).then_inc(finished, 16)
                sp.dma_start(out[N - tail_nodes:N, :].rearrange("(a k) f -> a (k f)", a=1),
                             xs[tail_parts:tail_parts + 1, full_blocks, 0:tail_nodes * D]).then_inc(finished, 16)
                sp.wait_ge(finished, 48)


def edge_phase(nc, sem, layer, acc, table, idx, rel_dst, base_row, passes, iota, window_iota, ident,
               ident_bf, w_edge, edge_attr):
    name = f"edge{layer}_"
    mlp = layer == 2
    width = H if mlp else D
    sums = D + FE + 1 if layer == 0 else width
    idx_ready = sem(name + "idx_ready")
    idx_taken = sem(name + "idx_taken")
    gathered = [sem(name + f"gathered{j}") for j in range(SLOTS)]
    sel_ready = sem(name + "sel_ready")
    summed = sem(name + "summed")
    acc_added = sem(name + "acc_added")
    cleared = sem(name + "cleared")
    shifted = sem(name + "shifted")
    if layer in (0, 2):
        attr_in = [sem(name + f"attr_in{j}") for j in range(SLOTS)]
    if layer == 0:
        attr_ready = sem(name + "attr_ready")
    if mlp:
        rcv_in = [sem(name + f"rcv_in{j}") for j in range(SLOTS)]
        flipped = sem(name + "flipped")
        flip_ready = sem(name + "flip_ready")
        pre_ready = sem(name + "pre_ready")
        pre_added = sem(name + "pre_added")
        relu_ready = sem(name + "relu_ready")

    with ExitStack() as scope:
        def sb(n, shape, dt=F32):
            return scope.enter_context(nc.sbuf_tensor(name + n, shape, dt))

        def ps(n, dt=F32):
            return scope.enter_context(nc.psum_tensor(name + n, [P, 512], dt))

        idx_slot = [sb(f"idx{j}", [P, TILES], I32) for j in range(SLOTS)]
        msg_w = P if layer == 0 else width
        msg = [sb(f"msg{j}", [P, TILES, msg_w]) for j in range(SLOTS)]
        sel = [sb(f"sel{j}", [P, TILES, P]) for j in range(SLOTS)]
        attr = [sb(f"attr{j}", [P, TILES * FE]) for j in range(SLOTS)] if layer in (0, 2) else None
        sum_ps = [ps(f"sum_ps{i}") for i in range(2)]
        if mlp:
            sel_bf = [sb(f"sel_bf{j}", [P, TILES, P], BF16) for j in range(SLOTS)]
            sel_t = [sb(f"sel_t{i}", [P, TILES * P]) for i in range(2)]
            attr_t = [sb(f"attr_t{i}", [P, P]) for i in range(2)]
            rcv = [sb(f"rcv{j}", [P, H]) for j in range(SLOTS)]
            hid = [sb(f"hid{j}", [P, TILES * H]) for j in range(SLOTS)]
            sel_ps = ps("sel_ps", BF16)
            attr_ps = ps("attr_ps")
            pre_ps = [ps(f"pre_ps{i}") for i in range(2)]

        def load_passes(eng):
            return eng.value_load(passes[0:1, 0:1], min_val=1, max_val=MAX_PASSES)

        def load_bases(engine_type, p, i):
            _, values = nc.values_load_multi_w_load_instructions(
                base_row[0:1, bass.ds(i * SLOTS, SLOTS)], engines=[engine_type], min_val=0, max_val=N - 1)
            return [nc.s_assert_within(v + p * P, min_val=0, max_val=N - 1,
                                       skip_runtime_bounds_check_because="the table is zero where p is not")
                    for v in values]

        with nc.Block() as block:
            @block.gpsimd
            def _(pool):
                of = table[0] if mlp else table
                with pool.Fori(0, load_passes(pool)) as p:
                    with pool.Fori(0, ITERS) as i:
                        n = p * ITERS + i
                        for j in range(SLOTS):
                            pool.wait_ge(idx_ready, n * SLOTS + j + 1)
                            pool.sem_inc(idx_taken, 1)
                            for u in range(TILES):
                                nc.gpsimd.indirect_dma_start(
                                    msg[j][:, u, 0:width], None, of,
                                    bass.IndirectOffsetOnAxis(ap=idx_slot[j][:, u:u + 1], axis=0),
                                ).then_inc(gathered[j], 16)

            @block.sync
            def _(sp):
                if attr is None:
                    return

                def load_attr(j, rows, parts, n):
                    sp.wait_ge(flipped if mlp else attr_ready, n * SLOTS + j + 1)
                    sp.dma_start(attr[j][0:parts, :], rows).then_inc(attr_in[j], 16)

                def load_receivers(j, base, n):
                    sp.wait_ge(pre_ready, n * SLOTS + j + 1)
                    sp.dma_start(rcv[j][:, :], table[1][bass.ds(base, P), :]).then_inc(rcv_in[j], 16)

                full = E // GE
                tail_parts = (E - full * GE) // TILES
                groups = edge_attr[0:full * GE, :].rearrange("(g p u) f -> g p (u f)", p=P, u=TILES)
                with sp.Fori(0, load_passes(sp)) as p:
                    with sp.Fori(0, ITERS - 1) as i:
                        n = p * ITERS + i
                        bases = load_bases(SP_ENGINE, p, i) if mlp else None
                        for j in range(SLOTS):
                            load_attr(j, groups[bass.ds(i * SLOTS + j, 1)].rearrange("a p f -> (a p) f"), P, n)
                            if mlp:
                                load_receivers(j, bases[j], n)
                    n = p * ITERS + (ITERS - 1)
                    bases = load_bases(SP_ENGINE, p, ITERS - 1) if mlp else None
                    for j in range(SLOTS):
                        g = (ITERS - 1) * SLOTS + j
                        if g == full:
                            load_attr(j, edge_attr[full * GE:E, :].rearrange("(p u) f -> p (u f)", u=TILES),
                                      tail_parts, n)
                        else:
                            load_attr(j, groups[min(g, full - 1)], P, n)
                        if mlp:
                            load_receivers(j, bases[j], n)

            @block.scalar
            def _(act):
                if mlp:
                    act.sem_inc(flip_ready, 2)
                if layer == 0:
                    act.sem_inc(attr_ready, SLOTS)
                    for j in range(SLOTS):
                        nc.scalar.activation(msg[j][:, :, D + FE:D + FE + 1],
                                             ident[:, 0:TILES].unsqueeze(2), ACT.Copy, bias=1.0, scale=0.0)

                def give_indices(n, i, j):
                    act.wait_ge(pre_added if mlp else summed, n * SLOTS + j + 1)
                    nc.scalar.copy(idx_slot[j][:, :],
                                   idx[:, bass.ds((i * SLOTS + j) * TILES, TILES)]).then_inc(idx_ready, 1)

                def place_attr(n, j):
                    act.wait_ge(attr_in[j], n * 16 + 16)
                    nc.scalar.copy(msg[j][:, :, D:D + FE],
                                   attr[j][:, :].rearrange("p (u f) -> p u f", u=TILES)).then_inc(attr_ready, 1)

                def copy_flipped(n, j):
                    act.wait_ge(flipped, n * SLOTS + j + 1 + SLOTS)
                    act.wait_ge(pre_ready, n * SLOTS + j + 3)
                    nc.scalar.copy(attr_t[j % 2][:, :], attr_ps[:, 0:P])
                    nc.scalar.copy(sel_t[j % 2][:, :], sel_ps[:, :]).then_inc(flip_ready, 1)

                def relu(n, j):
                    act.wait_ge(pre_added, n * SLOTS + j + 1 + SLOTS)
                    nc.scalar.activation(hid[j][:, :], hid[j][:, :], ACT.Relu).then_inc(relu_ready, 1)

                ahead = 2
                with act.Fori(0, load_passes(act)) as p:
                    def group(i, j, last, first):
                        n = p * ITERS + i
                        if j + ahead < SLOTS:
                            give_indices(n, i, j + ahead)
                        elif not last:
                            give_indices(n + 1, i + 1, j + ahead - SLOTS)
                        if layer == 0:
                            place_attr(n, j)
                        if mlp:
                            copy_flipped(n, j)
                            if j > 0:
                                relu(n, j - 1)
                            elif not first:
                                relu(n + (-1), SLOTS - 1)

                    for j in range(ahead):
                        give_indices(p * ITERS, 0, j)
                    for j in range(SLOTS):
                        group(0, j, False, True)
                    with act.Fori(1, ITERS - 1) as i:
                        for j in range(SLOTS):
                            group(i, j, False, False)
                    for j in range(SLOTS):
                        group(ITERS - 1, j, True, False)
                    if mlp:
                        relu(p * ITERS + (ITERS - 1), SLOTS - 1)

            @block.vector
            def _(dve):
                nc.vector.tensor_copy(window_iota[:, :], iota[:, :]).then_inc(shifted, 1)
                nc.vector.memset(acc[0:sums, :], 0.0).then_inc(cleared, 1)
                dve.sem_inc(acc_added, 2)
                if mlp:
                    dve.sem_inc(pre_added, SLOTS)

                def select(n, i, j):
                    dve.wait_ge(summed, n * SLOTS + j + 1)
                    rel = rel_dst[:, bass.ds((i * SLOTS + j) * TILES, TILES)]
                    nc.vector.tensor_tensor(sel[j][:, :, :], rel.unsqueeze(2).to_broadcast([P, TILES, P]),
                                            window_iota[:, :].unsqueeze(1).to_broadcast([P, TILES, P]),
                                            ALU.is_equal).then_inc(sel_ready, 1)
                    if mlp:
                        dve.wait_ge(sel_ready, (n * SLOTS + j) * 2 + 1)
                        nc.vector.tensor_copy(sel_bf[j][:, :, :], sel[j][:, :, :]).then_inc(sel_ready, 1)

                def add_sender(n, j):
                    dve.wait_ge(pre_ready, n * SLOTS + j + 1 + SLOTS)
                    dve.wait_ge(gathered[j], n * 64 + 64)
                    nc.vector.tensor_tensor(hid[j][:, :], pre_ps[j % 2][:, :],
                                            msg[j][:, :, :].rearrange("p u f -> p (u f)"),
                                            ALU.add).then_inc(pre_added, 1)

                def add_sums(n, j, base):
                    dve.wait_ge(summed, n * SLOTS + j + 1 + SLOTS)
                    dve.wait_ge(acc_added, n * SLOTS + j + 2)
                    to = acc[0:sums, bass.ds(base, P)]
                    nc.vector.tensor_tensor(to, to, sum_ps[j % 2][0:sums, 0:P], ALU.add).then_inc(acc_added, 1)

                behind = 2 if mlp else 1
                dve.wait_ge(shifted, 1)
                dve.wait_ge(cleared, 1)
                with dve.Fori(0, load_passes(dve)) as p:
                    def iteration(i, first):
                        n = p * ITERS + i
                        if not first:
                            before = load_bases(DVE_ENGINE, p, i + (-1))
                        bases = load_bases(DVE_ENGINE, p, i)
                        for j in range(SLOTS):
                            select(n, i, j)
                            if mlp:
                                if j > 0:
                                    add_sender(n, j - 1)
                                elif not first:
                                    add_sender(n + (-1), SLOTS - 1)
                            if j >= behind:
                                add_sums(n, j - behind, bases[j - behind])
                            elif not first:
                                add_sums(n + (-1), SLOTS + j - behind, before[SLOTS + j - behind])

                    iteration(0, True)
                    with dve.Fori(1, ITERS) as i:
                        iteration(i, False)
                    n = p * ITERS + (ITERS - 1)
                    bases = load_bases(DVE_ENGINE, p, ITERS - 1)
                    if mlp:
                        add_sender(n, SLOTS - 1)
                    for j in range(SLOTS - behind, SLOTS):
                        add_sums(n, j, bases[j])
                    nc.vector.tensor_scalar(window_iota[:, :], window_iota[:, :], float(P), None,
                                            ALU.add).then_inc(shifted, 1)
                    dve.wait_ge(shifted, p + 2)

            @block.tensor
            def _(pe):
                pe.sem_inc(summed, SLOTS)
                if mlp:
                    pe.sem_inc(flipped, SLOTS)
                    pe.sem_inc(pre_ready, SLOTS)

                def flip(n, j):
                    pe.wait_ge(sel_ready, (n * SLOTS + j) * 2 + 2)
                    pe.wait_ge(attr_in[j], n * 16 + 16)
                    pe.wait_ge(flip_ready, n * SLOTS + j + 2)
                    for u in range(TILES):
                        nc.tensor.transpose(sel_ps[:, u * P:(u + 1) * P], sel_bf[j][:, u, :], ident_bf[:, :])
                    nc.tensor.transpose(attr_ps[:, 0:P], attr[j][:, :], ident[:, :]).then_inc(flipped, 1)

                def hidden(n, j):
                    pe.wait_ge(flip_ready, n * SLOTS + j + 3)
                    pe.wait_ge(rcv_in[j], n * 16 + 16)
                    pe.wait_ge(pre_added, n * SLOTS + j + 3)
                    nc.tensor.matmul(pre_ps[j % 2][:, :], attr_t[j % 2][:, :], w_edge[:, :], start=True,
                                     stop=False)
                    for u in range(TILES):
                        last = nc.tensor.matmul(pre_ps[j % 2][:, u * H:(u + 1) * H],
                                                sel_t[j % 2][:, u * P:(u + 1) * P], rcv[j][:, :],
                                                start=False, stop=u == TILES - 1)
                    last.then_inc(pre_ready, 1)

                def sum_up(n, j):
                    pe.wait_ge(acc_added, n * SLOTS + j + 1)
                    if mlp:
                        pe.wait_ge(relu_ready, n * SLOTS + j + 1)
                    else:
                        pe.wait_ge(sel_ready, n * SLOTS + j + 1)
                        pe.wait_ge(gathered[j], n * 64 + 64)
                    if layer == 0:
                        pe.wait_ge(attr_ready, n * SLOTS + j + 1 + SLOTS)
                    for u in range(TILES):
                        lhs = hid[j][:, u * H:(u + 1) * H] if mlp else msg[j][:, u, 0:sums]
                        last = nc.tensor.matmul(sum_ps[j % 2][0:sums, 0:P], lhs, sel[j][:, u, :], start=u == 0,
                                                stop=u == TILES - 1)
                    last.then_inc(summed, 1)

                with pe.Fori(0, load_passes(pe)) as p:
                    def iteration(i, first):
                        n = p * ITERS + i
                        for j in range(SLOTS):
                            if not mlp:
                                sum_up(n, j)
                                continue
                            flip(n, j)
                            if j >= 1:
                                hidden(n, j - 1)
                            elif not first:
                                hidden(n + (-1), SLOTS - 1)
                            if j >= 2:
                                sum_up(n, j - 2)
                            elif not first:
                                sum_up(n + (-1), SLOTS + j - 2)

                    if mlp:
                        iteration(0, True)
                        with pe.Fori(1, ITERS) as i:
                            iteration(i, False)
                        n = p * ITERS + (ITERS - 1)
                        hidden(n, SLOTS - 1)
                        for j in range(SLOTS - 2, SLOTS):
                            sum_up(n, j)
                    else:
                        with pe.Fori(0, ITERS) as i:
                            iteration(i, False)


_INS = ["x", "src", "dst", "edge_attr_32", "edge_type_16", "L0_gnn_weight", "L0_gnn_h_bias",
        "L0_gnn_loop_weight", "L1_gnn_W", "L1_gnn_b", "L2_gnn_W1", "L2_gnn_b1", "L2_gnn_W2", "L2_gnn_b2",
        "L2_gnn_Wn", "L2_gnn_bn", "L3_gnn_W1", "L3_gnn_b1", "L3_gnn_W2", "L3_gnn_b2"]


def kernel(**inputs):
    import numpy as _np
    import concourse.bacc as _bacc
    from concourse import mybir as _mybir
    from concourse.bass_utils import run_bass_kernel_spmd as _run

    nc = _bacc.Bacc("TRN2", target_bir_lowering=False, num_devices=1)
    arrays, args = {}, []
    for name in _INS:
        a = _np.ascontiguousarray(inputs[name])
        arrays[f"in_{name}_dram"] = a
        args.append(nc.dram_tensor(f"in_{name}_dram", a.shape, _mybir.dt.from_np(a.dtype),
                                   kind="ExternalInput").ap())
    out = nc.dram_tensor("out_0_dram", (N, D), _mybir.dt.float32, kind="ExternalOutput").ap()
    gnn_program(nc, *args, out)
    r = _run(nc, [arrays], core_ids=[0])
    return r.results[0]["out_0_dram"]
```

```python
from contextlib import ExitStack

import concourse.bass as bass
from concourse import mybir

F32 = mybir.dt.float32
BF16 = mybir.dt.bfloat16
I32 = mybir.dt.int32
ALU = mybir.AluOpType
ACT = mybir.ActivationFunctionType
AX = mybir.AxisListType
DVE_ENGINE = mybir.EngineType.DVE
SP_ENGINE = mybir.EngineType.SP
ACT_ENGINE = mybir.EngineType.Activation
PE_ENGINE = mybir.EngineType.PE

P = 128
D = 64
FE = 32
H = 128
RELS = 16
N = 12500
E = 200000

KW = 7
BLK = P * KW
NB = -(-N // BLK)
NPAD = NB * BLK
ACC_W = NPAD + P
PAIRS = NB // 2

TILES = 4
GE = P * TILES
PER = 8
SLOTS = 4
ITERS = -(-E // (GE * PER))
G = ITERS * PER
CH = -(-G // P)
PAD_DST = -1000000.0
MAX_PASSES = -(-N // P)
EPS = 1e-5

assert NB % 2 == 0 and GE == 512


def gnn_program(nc, x, src, dst, edge_attr, edge_type, w_rel, b_rel, w_loop, w_sum, b_sum,
                w1_mlp, b1_mlp, w2_mlp, b2_mlp, wn_mlp, bn_mlp, w1_lin, b1_lin, w2_lin, b2_lin, out):
    rel_table = nc.dram_tensor("rel_table", [NPAD * RELS, D], F32).ap()
    h1_table = nc.dram_tensor("h1_table", [NPAD, D], F32).ap()
    snd_table = nc.dram_tensor("snd_table", [NPAD, H], F32).ap()
    rcv_table = nc.dram_tensor("rcv_table", [ACC_W, H], F32).ap()
    h3_table = nc.dram_tensor("h3_table", [NPAD, D], F32).ap()

    with ExitStack() as ctx:
        def sb(name, shape, dt=F32, scope=ctx):
            return scope.enter_context(nc.sbuf_tensor(name, shape, dt))

        held = []

        def sem(name):
            held.append(nc.alloc_semaphore(name=name))
            return held[-1]

        def end_phase():
            nc.clear_and_free_semaphores(held)
            held.clear()
            nc.all_engine_barrier()

        xs = sb("xs", [P, NB, KW * D])
        acc = sb("acc", [P, ACC_W])
        rel_dst = sb("rel_dst", [P, G * TILES])
        idx_src = sb("idx_src", [P, (G + PER) * TILES], I32)
        idx_rel = sb("idx_rel", [P, (G + PER) * TILES], I32)
        base_row = sb("base_row", [1, CH * P], I32)
        schedule = sb("schedule", [1, NB + 1], I32)
        passes = sb("passes", [1, 1], I32)
        iota = sb("iota", [P, P])
        window_iota = sb("window_iota", [P, P])
        ident = sb("ident", [P, P])
        ident_bf = sb("ident_bf", [P, P], BF16)
        wc1 = sb("wc1", [D + 1, D])
        wc2 = sb("wc2", [D + 1, D + 2 * H])
        wc3 = sb("wc3", [D + 1, D])
        wp0 = sb("wp0", [D + 1, D])
        wp1 = sb("wp1", [D, D])
        wp2 = sb("wp2", [H, D + 1])
        wp2_deg = sb("wp2_deg", [D + FE + 1, D + 1])
        wp3a = sb("wp3a", [D + FE + 1, H])
        wp3b = sb("wp3b", [H, D])
        w_edge = sb("w_edge", [P, TILES * H])

        with ExitStack() as early:
            w0_parts = sb("w0_parts", [P, 3, D + RELS * D], BF16, early)
            setup(nc, sem, locals())
            end_phase()
            first_nodes(nc, sem, xs, w0_parts, rel_table, ident)
            end_phase()
        hidden_acc = sb("hidden_acc", [P, ACC_W])

        env = locals()
        env["own_weights"] = [None, wc1, wc2, wc3, None]
        env["sum_weights"] = [wp0, wp1, wp2, wp3a]
        env["tables"] = [rel_table, h1_table, (snd_table, rcv_table), h3_table, None]
        for layer in range(4):
            layer_phase(nc, sem, layer, env)
            if layer < 3:
                end_phase()


def setup(nc, sem, env):
    x, src, dst, edge_type = env["x"], env["src"], env["dst"], env["edge_type"]
    xs, ident, iota, ident_bf = env["xs"], env["ident"], env["iota"], env["ident_bf"]
    wc1, wc2, wc3, wp0, w0_parts = env["wc1"], env["wc2"], env["wc3"], env["wp0"], env["w0_parts"]
    schedule = env["schedule"]
    wp1, wp2, wp2_deg, wp3a, wp3b = env["wp1"], env["wp2"], env["wp2_deg"], env["wp3a"], env["wp3b"]
    w_edge, acc, base_row, passes = env["w_edge"], env["acc"], env["base_row"], env["passes"]

    zeroed = sem("setup_zeroed")
    const_ready = sem("setup_const_ready")
    loaded = sem("setup_loaded")
    chain = sem("setup_chain")
    bad_ready = sem("setup_bad_ready")
    bad_summed = sem("setup_bad_summed")
    lists_ready = sem("setup_lists_ready")
    ready_made = sem("setup_ready_made")
    turned = sem("setup_turned")
    evacuated = sem("setup_evacuated")

    with ExitStack() as scope:
        def sb(name, shape, dt=F32):
            return scope.enter_context(nc.sbuf_tensor(name, shape, dt))

        raw_dst = sb("raw_dst", [P, CH, GE], I32)
        raw_src = sb("raw_src", [P, CH, GE], I32)
        raw_typ = sb("raw_typ", [P, CH, GE], I32)
        dst_f = sb("dst_f", [P, CH, GE])
        src_f = sb("src_f", [P, CH, GE])
        row_f = sb("row_f", [P, CH, GE])
        off_f = sb("off_f", [P, CH, GE])
        real = sb("real", [P, CH, GE])
        bad = sb("bad", [P, CH, GE])
        first = sb("first", [P, CH])
        base_f = sb("base_f", [P, CH])
        any_bad = sb("any_bad", [P, 1])
        fast = sb("fast", [P, 1])
        ones = sb("ones", [P, P])
        part = sb("part", [P, 1])
        w_sum_raw = sb("w_sum_raw", [D, 2 * D])
        w0 = sb("w0", [P, D + RELS * D])
        base_wide = sb("base_wide", [P, CH, NB])
        block_end = sb("block_end", [P, 1])
        iteration = sb("iteration", [NB, G])
        touched = sb("touched", [NB, G])
        ready = sb("ready", [NB, 1])
        turn_ps = [scope.enter_context(nc.psum_tensor(f"turn_ps{i}", [P, 512], F32)) for i in range(4)]
        row_ps = scope.enter_context(nc.psum_tensor("row_ps", [P, 512], F32))
        sum_ps = scope.enter_context(nc.psum_tensor("sum_ps", [P, 512], F32))
        w_ps = scope.enter_context(nc.psum_tensor("w_ps", [P, 512], F32))

        full_rows = E // (P * GE) * P * GE
        tail_rows = (E - full_rows) // GE
        tail_edges = E - full_rows - tail_rows * GE
        full_blocks = N // BLK
        tail_parts = (N - full_blocks * BLK) // KW
        tail_nodes = N - full_blocks * BLK - tail_parts * KW
        lists = [(env["rel_dst"], off_f), (env["idx_src"], src_f), (env["idx_rel"], row_f)]

        with nc.Block() as block:
            @block.gpsimd
            def _(pool):
                nc.gpsimd.memset(raw_dst[:, CH - 1, :], int(PAD_DST)).then_inc(zeroed, 1)
                nc.gpsimd.memset(raw_src[:, CH - 1, :], 0).then_inc(zeroed, 1)
                nc.gpsimd.memset(raw_typ[:, CH - 1, :], 0).then_inc(zeroed, 1)
                nc.gpsimd.memset(xs[:, NB - 1, :], 0.0).then_inc(zeroed, 1)
                nc.gpsimd.memset(w_edge[:, :], 0.0).then_inc(zeroed, 1)
                nc.gpsimd.memset(wc2[:, :], 0.0).then_inc(zeroed, 1)
                nc.gpsimd.memset(wp2[:, :], 0.0).then_inc(zeroed, 1)
                nc.gpsimd.memset(wp2_deg[:, :], 1.0).then_inc(zeroed, 1)
                nc.gpsimd.iota(iota[:, :], [[1, P]], base=0, channel_multiplier=0,
                               allow_small_or_imprecise_dtypes=True).then_inc(const_ready, 1)
                nc.gpsimd.iota(part[:, :], [[0, 1]], base=0, channel_multiplier=1,
                               allow_small_or_imprecise_dtypes=True).then_inc(const_ready, 1)
                nc.gpsimd.iota(block_end[:, :], [[0, 1]], base=BLK, channel_multiplier=BLK,
                               allow_small_or_imprecise_dtypes=True).then_inc(const_ready, 1)
                nc.gpsimd.iota(iteration[:, :].rearrange("b (i g) -> b i g", g=PER), [[1, ITERS], [0, PER]],
                               base=1, channel_multiplier=0,
                               allow_small_or_imprecise_dtypes=True).then_inc(const_ready, 1)
                nc.gpsimd.memset(ones[:, :], 1.0).then_inc(const_ready, 1)

            @block.sync
            def _(sp):
                loads = []
                sp.wait_ge(zeroed, 8)
                for raw, edges in ((raw_dst, dst), (raw_src, src), (raw_typ, edge_type)):
                    loads.append((raw[:, 0:CH - 1, :],
                                  edges[0:full_rows].rearrange("(c g e) -> g c e", g=P, e=GE)))
                    loads.append((raw[0:tail_rows, CH - 1, :],
                                  edges[full_rows:full_rows + tail_rows * GE].rearrange("(g e) -> g e", e=GE)))
                    loads.append((raw[tail_rows:tail_rows + 1, CH - 1, 0:tail_edges],
                                  edges[E - tail_edges:E].rearrange("(a e) -> a e", a=1)))
                n0 = full_blocks * BLK
                loads.append((xs[:, 0:full_blocks, :],
                              x[0:n0, :].rearrange("(b p k) f -> p b (k f)", p=P, k=KW)))
                loads.append((xs[0:tail_parts, full_blocks, :],
                              x[n0:n0 + tail_parts * KW, :].rearrange("(p k) f -> p (k f)", k=KW)))
                loads.append((xs[tail_parts:tail_parts + 1, full_blocks, 0:tail_nodes * D],
                              x[N - tail_nodes:N, :].rearrange("(a k) f -> a (k f)", a=1)))
                bias = lambda b: b.rearrange("(a f) -> a f", a=1)
                for half in range(2):
                    rows = w0[half * D:(half + 1) * D, :]
                    loads.append((rows[:, 0:D], env["w_loop"]))
                    loads.append((rows[:, D:].rearrange("i (r o) -> i r o", r=RELS),
                                  env["w_rel"].rearrange("r i o -> i r o")))
                loads.append((wp0[D:D + 1, 0:D], bias(env["b_rel"])))
                loads.append((w_sum_raw[:, :], env["w_sum"]))
                loads.append((wc1[D:D + 1, :], bias(env["b_sum"])))
                loads.append((wc2[0:D, 0:D], env["wn_mlp"]))
                loads.append((wc2[0:D, D:D + H], env["w1_mlp"][0:D, :]))
                loads.append((wc2[0:D, D + H:], env["w1_mlp"][D:2 * D, :]))
                loads.append((wc2[D:D + 1, 0:D], bias(env["bn_mlp"])))
                loads.append((wc2[D:D + 1, D + H:], bias(env["b1_mlp"])))
                for u in range(TILES):
                    loads.append((w_edge[FE * u:FE * u + FE, H * u:H * u + H], env["w1_mlp"][2 * D:, :]))
                loads.append((wp2[:, 0:D], env["w2_mlp"]))
                loads.append((wp2_deg[D + FE:D + FE + 1, 0:D], bias(env["b2_mlp"])))
                loads.append((wc3[0:D, :], env["w2_lin"][0:D, :]))
                loads.append((wc3[D:D + 1, :], bias(env["b2_lin"])))
                loads.append((wp3a[0:D + FE, :], env["w1_lin"]))
                loads.append((wp3a[D + FE:D + FE + 1, :], bias(env["b1_lin"])))
                loads.append((wp3b[:, :], env["w2_lin"][D:, :]))
                for to, of in loads:
                    sp.dma_start(to, of).then_inc(loaded, 16)
                sp.wait_ge(loaded, 16 * len(loads))
                sp.sem_inc(loaded, 1)

            n_loads = 9 + 3 + 12 + TILES + 7
            all_loaded = 16 * n_loads + 1

            @block.vector
            def _(dve):
                done = [0]

                def link(ins):
                    done[0] += 1
                    ins.then_inc(chain, 1)
                    dve.wait_ge(chain, done[0])

                dve.wait_ge(const_ready, 5)
                link(nc.vector.tensor_scalar(ident[:, :], iota[:, :], part[:, 0:1], None, ALU.is_equal))
                link(nc.vector.tensor_copy(ident_bf[:, :], ident[:, :]))
                dve.wait_ge(loaded, all_loaded)
                nc.vector.tensor_copy(src_f[:, :, :], raw_src[:, :, :])
                nc.vector.tensor_copy(dst_f[:, :, :], raw_dst[:, :, :])
                link(nc.vector.tensor_copy(row_f[:, :, :], raw_typ[:, :, :]))
                link(nc.vector.scalar_tensor_tensor(out=row_f[:, :, :], in0=src_f[:, :, :],
                                                    scalar=float(RELS), in1=row_f[:, :, :],
                                                    op0=ALU.mult, op1=ALU.add))
                link(nc.vector.tensor_scalar(base_f[:, :], dst_f[:, :, 0], 0.0, float(N - 1), ALU.is_lt,
                                             ALU.mult))
                link(nc.vector.scalar_tensor_tensor(out=first[:, :], in0=dst_f[:, :, 0], scalar=0.0,
                                                    in1=base_f[:, :], op0=ALU.max, op1=ALU.add))

                def spread(t):
                    return t[:, :].unsqueeze(2).to_broadcast([P, CH, GE])

                nc.vector.tensor_scalar(real[:, :, :], dst_f[:, :, :], 0.0, None, ALU.is_ge)
                link(nc.vector.tensor_tensor(off_f[:, :, :], dst_f[:, :, :], spread(first), ALU.subtract))
                link(nc.vector.scalar_tensor_tensor(out=real[:, :, :], in0=off_f[:, :, :], scalar=0.0,
                                                    in1=real[:, :, :], op0=ALU.is_lt, op1=ALU.mult))
                link(nc.vector.scalar_tensor_tensor(out=bad[:, :, :], in0=off_f[:, :, :], scalar=float(P),
                                                    in1=real[:, :, :], op0=ALU.is_ge, op1=ALU.add))
                nc.vector.tensor_reduce(any_bad[:, :], bad[:, :, :], AX.XY, ALU.max).then_inc(bad_ready, 1)
                dve.wait_ge(bad_summed, 1)
                link(nc.vector.tensor_scalar(fast[:, :], sum_ps[:, 0:1], 0.0, None, ALU.is_equal))
                nc.vector.tensor_scalar(passes[:, :], fast[0:1, :], float(1 - MAX_PASSES), float(MAX_PASSES),
                                        ALU.mult, ALU.add)
                link(nc.vector.tensor_scalar(base_f[:, :], first[:, :], fast[:, 0:1], None, ALU.mult))
                link(nc.vector.tensor_copy(base_wide[:, :, :],
                                           base_f[:, :].unsqueeze(2).to_broadcast([P, CH, NB])))
                nc.vector.tensor_tensor(off_f[:, :, :], dst_f[:, :, :], spread(base_f),
                                        ALU.subtract).then_inc(lists_ready, 1)
                link(nc.vector.tensor_copy(w0_parts[:, 0, :], w0[:, :]))
                link(nc.vector.tensor_tensor(w0[:, :], w0[:, :], w0_parts[:, 0, :], ALU.subtract))
                link(nc.vector.tensor_copy(w0_parts[:, 1, :], w0[:, :]))
                nc.vector.tensor_tensor(w0_parts[0:D, 2, :], w0[0:D, :], w0_parts[0:D, 1, :], ALU.subtract)
                nc.vector.tensor_copy(w0_parts[D:P, 2, :], w0_parts[D:P, 0, :])
                nc.vector.tensor_copy(wp0[0:D, :], ident[0:D, 0:D])
                dve.wait_ge(turned, len(lists) * CH + 1)
                nc.vector.tensor_copy(base_row[:, :], row_ps[0:1, 0:CH * P])
                link(nc.vector.scalar_tensor_tensor(out=touched[:, :], in0=row_ps[0:NB, 0:G],
                                                    scalar=block_end[0:NB, 0:1], in1=iteration[:, :],
                                                    op0=ALU.is_lt, op1=ALU.mult))
                nc.vector.tensor_reduce(ready[:, :], touched[:, :], AX.X, ALU.max).then_inc(ready_made, 1)
                dve.wait_ge(turned, len(lists) * CH + 3)
                nc.vector.tensor_copy(wc1[0:D, :], w_ps[0:D, 0:D])
                nc.vector.tensor_copy(wp1[:, :], w_ps[0:D, D:2 * D])
                nc.vector.memset(schedule[:, 0:1], 0)
                dve.wait_ge(turned, len(lists) * CH + 4)
                nc.vector.tensor_copy(schedule[:, 1:NB + 1], sum_ps[0:1, 64:64 + NB])

            @block.tensor
            def _(pe):
                pe.wait_ge(bad_ready, 1)
                nc.tensor.matmul(sum_ps[:, 0:1], ones[:, :], any_bad[:, :], start=True,
                                 stop=True).then_inc(bad_summed, 1)
                pe.wait_ge(lists_ready, 1)
                for a, (_, laid) in enumerate(lists):
                    for c in range(CH):
                        n = a * CH + c
                        if n >= 4:
                            pe.wait_ge(evacuated, n - 3)
                        view = laid[:, c, :].rearrange("g (p u) -> g u p", u=TILES)
                        for u in range(TILES):
                            last = nc.tensor.transpose(turn_ps[n % 4][:, u * P:(u + 1) * P], view[:, u, :],
                                                       ident[:, :])
                        last.then_inc(turned, 1)
                for c in range(CH):
                    last = nc.tensor.matmul(row_ps[0:NB, c * P:(c + 1) * P], base_wide[:, c, :], ident[:, :],
                                            start=True, stop=True)
                last.then_inc(turned, 1)
                for half in range(2):
                    nc.tensor.transpose(w_ps[0:D, half * D:(half + 1) * D],
                                        w_sum_raw[:, half * D:(half + 1) * D],
                                        ident[0:D, 0:D]).then_inc(turned, 1)
                pe.wait_ge(ready_made, 1)
                nc.tensor.matmul(sum_ps[0:1, 64:64 + NB], ready[:, :], ident[0:NB, 0:NB], start=True,
                                 stop=True).then_inc(turned, 1)

            @block.scalar
            def _(act):
                for n in range(len(lists) * CH):
                    to, c = lists[n // CH][0], n % CH
                    groups = min(P, G - c * P)
                    act.wait_ge(turned, n + 1)
                    turned_lists = turn_ps[n % 4][:, :].rearrange("p (u g) -> p u g", u=TILES)
                    if c == 0 and n > 0:
                        nc.scalar.copy(
                            to[:, G * TILES:(G + PER) * TILES].rearrange("p (g u) -> p u g", u=TILES),
                            turned_lists[:, :, 0:PER])
                    nc.scalar.copy(
                        to[:, c * GE:c * GE + groups * TILES].rearrange("p (g u) -> p u g", u=TILES),
                        turned_lists[:, :, 0:groups]).then_inc(evacuated, 1)


def first_nodes(nc, sem, xs, w0_parts, table, ident):
    step = sem("first_step")
    var_ready = sem("first_var_ready")
    std_ready = sem("first_std_ready")
    h_ready = sem("first_h_ready")
    turn_begun = sem("first_turn_begun")
    turned = sem("first_turned")
    high_ready = sem("first_high_ready")
    copy_begun = sem("first_copy_begun")
    high_copied = sem("first_high_copied")
    low_ready = sem("first_low_ready")
    own_ready = sem("first_own_ready")
    own_added = sem("first_own_added")
    rows_ready = sem("first_rows_ready")
    rows_copied = sem("first_rows_copied")
    stored = [sem(f"first_stored{i}") for i in range(2)]
    STEPS = 11

    with ExitStack() as scope:
        def sb(n, shape, dt=F32):
            return scope.enter_context(nc.sbuf_tensor("first_" + n, shape, dt))

        def ps(n, shape):
            return scope.enter_context(nc.psum_tensor("first_" + n, shape, F32))

        mean = sb("mean", [P, KW])
        rstd = sb("rstd", [P, KW])
        xc = sb("xc", [P, KW, D])
        sq = sb("sq", [P, KW, D])
        h = [sb(f"h{i}", [P, KW, D]) for i in range(2)]
        ht_ab = [sb(f"ht_ab{i}", [P, BLK], BF16) for i in range(2)]
        ht_ac = [sb(f"ht_ac{i}", [P, BLK], BF16) for i in range(2)]
        rest = sb("rest", [P, BLK])
        rows = [sb(f"rows{i}", [P, RELS * D]) for i in range(2)]
        own_ps = ps("own_ps", [P, 512])
        ht_ps = ps("ht_ps", [P, 1024])
        row_ps = [ps(f"row_ps{i}", [P, 1024]) for i in range(2)]

        with nc.Block() as block:
            @block.tensor
            def _(pe):
                pe.sem_inc(turned, 2)
                pe.sem_inc(own_ready, 1)
                pe.sem_inc(rows_ready, 2 * KW)
                with pe.Fori(0, PAIRS) as q:
                    for s in range(2):
                        b = q * 2 + s
                        pe.wait_ge(h_ready, b + 1)
                        pe.wait_ge(low_ready, b + 1)
                        pe.sem_inc(turn_begun, 1)
                        for k in range(KW):
                            last = nc.tensor.transpose(ht_ps[0:D, k * P:(k + 1) * P], h[s][:, k, :],
                                                       ident[:, :])
                        last.then_inc(turned, 1)
                        pe.wait_ge(low_ready, b + 2)
                        pe.wait_ge(high_copied, b + 1)
                        pe.wait_ge(own_added, b + 1)

                        def project(to, k, c0, c1):
                            nodes = slice(k * P, (k + 1) * P)
                            nc.tensor.matmul(to, ht_ab[s][:, nodes], w0_parts[:, 0, c0:c1], start=True,
                                             stop=False)
                            nc.tensor.matmul(to, ht_ab[s][:, nodes], w0_parts[:, 1, c0:c1], start=False,
                                             stop=False)
                            return nc.tensor.matmul(to, ht_ac[s][:, nodes], w0_parts[:, 2, c0:c1],
                                                    start=False, stop=True)

                        for k in range(KW):
                            last = project(own_ps[:, k * D:(k + 1) * D], k, 0, D)
                        last.then_inc(own_ready, 1)
                        for k in range(KW):
                            slot = (s * KW + k) % 2
                            pe.wait_ge(rows_copied, b * KW + k + 1)
                            for c in range(0, RELS * D, 512):
                                last = project(row_ps[slot][:, c:c + 512], k, D + c, D + c + 512)
                            last.then_inc(rows_ready, 1)

            @block.scalar
            def _(act):
                act.sem_inc(rows_copied, 2)

                def root(b):
                    act.wait_ge(var_ready, b + 1)
                    nc.scalar.activation(rstd[:, :], rstd[:, :], ACT.Sqrt).then_inc(std_ready, 1)

                root(0)
                with act.Fori(0, PAIRS) as q:
                    for s in range(2):
                        b = q * 2 + s
                        act.wait_ge(rows_ready, (b + 1) * KW)
                        act.wait_ge(turned, b + 3)
                        nc.scalar.copy(ht_ab[s][0:D, :], ht_ps[0:D, 0:BLK]).then_inc(high_ready, 1)
                        for k in range(KW):
                            slot = (s * KW + k) % 2
                            act.wait_ge(rows_ready, b * KW + k + 1 + 2 * KW)
                            act.wait_ge(stored[slot], 16 * (q * KW + (s * KW + k) // 2 + 1))
                            nc.scalar.copy(rows[slot][:, :], row_ps[slot][:, :]).then_inc(rows_copied, 1)
                            if k == 1:
                                root(b + 1)

            @block.gpsimd
            def _(pool):
                with pool.Fori(0, PAIRS) as q:
                    for s in range(2):
                        b = q * 2 + s
                        pool.wait_ge(high_ready, b + 1)
                        pool.wait_ge(rows_ready, (b + 1) * KW)
                        pool.sem_inc(copy_begun, 1)
                        nc.gpsimd.tensor_copy(ht_ac[s][0:D, :], ht_ab[s][0:D, :]).then_inc(high_copied, 1)

            @block.vector
            def _(dve):
                dve.sem_inc(own_added, 1)
                dve.sem_inc(low_ready, 1)

                def linker(b, at):
                    done = [at]

                    def link(ins):
                        done[0] += 1
                        ins.then_inc(step, 1)
                        dve.wait_ge(step, b * STEPS + done[0])
                    return link

                def normalise(q, s):
                    b = q * 2 + s
                    xb = xs[:, bass.ds(b, 1), :].rearrange("p a (k f) -> p (a k) f", k=KW)
                    link = linker(b, 0)
                    norm_steps(nc, link, xb, mean[:, :], rstd[:, :], xc, sq)
                    dve.sem_inc(var_ready, 1)
                    dve.wait_ge(std_ready, b + 1)
                    link(nc.vector.reciprocal(rstd[:, :], rstd[:, :]))
                    dve.wait_ge(turned, b + 1)
                    link(nc.vector.scalar_tensor_tensor(
                        out=h[s][:, :, :], in0=xc[:, :, :], scalar=0.0,
                        in1=rstd[:, :].unsqueeze(2).to_broadcast([P, KW, D]), op0=ALU.max, op1=ALU.mult))
                    dve.sem_inc(h_ready, 1)

                def split(q, s):
                    b = q * 2 + s
                    link = linker(b, 8)
                    dve.wait_ge(high_ready, b + 1)
                    dve.wait_ge(rows_ready, (b + 1) * KW)
                    link(nc.vector.tensor_tensor(rest[D:P, :], ht_ps[0:D, 0:BLK], ht_ab[s][0:D, :],
                                                 ALU.subtract))
                    link(nc.vector.tensor_copy(ht_ab[s][D:P, :], rest[D:P, :]))
                    link(nc.vector.tensor_tensor(ht_ac[s][D:P, :], rest[D:P, :], ht_ab[s][D:P, :],
                                                 ALU.subtract))
                    dve.sem_inc(low_ready, 1)

                def add_own(b):
                    xb = xs[:, bass.ds(b, 1), :].rearrange("p a f -> p (a f)")
                    dve.wait_ge(own_ready, b + 2)
                    nc.vector.tensor_tensor(xb, xb, own_ps[:, 0:KW * D], ALU.add).then_inc(own_added, 1)

                normalise(0, 0)
                with dve.Fori(0, PAIRS - 1) as q:
                    split(q, 0)
                    normalise(q, 1)
                    add_own(q * 2)
                    split(q, 1)
                    normalise(q + 1, 0)
                    add_own(q * 2 + 1)
                split(PAIRS - 1, 0)
                normalise(PAIRS - 1, 1)
                add_own(NB - 2)
                split(PAIRS - 1, 1)
                dve.sem_inc(var_ready, 1)
                add_own(NB - 1)

            @block.sync
            def _(sp):
                to = table.rearrange("(b p k r) f -> b k p (r f)", p=P, k=KW, r=RELS)
                for s in range(2):
                    sp.sem_inc(stored[s], 16)
                with sp.Fori(0, PAIRS) as q:
                    for s in range(2):
                        b = q * 2 + s
                        for k in range(KW):
                            slot = (s * KW + k) % 2
                            sp.wait_ge(rows_copied, b * KW + k + 3)
                            sp.dma_start(to[bass.ds(b, 1), k].rearrange("a p f -> (a p) f"),
                                         rows[slot][:, :]).then_inc(stored[slot], 16)
                for s in range(2):
                    sp.wait_ge(stored[s], 16 * KW * PAIRS + 16)


def norm_steps(nc, link, xb, mean, var, xc, sq):
    link(nc.vector.tensor_reduce(mean, xb, AX.X, ALU.add))
    link(nc.vector.tensor_scalar(mean, mean, 1.0 / D, None, ALU.mult))
    link(nc.vector.tensor_tensor(xc[:, :, :], xb, mean.unsqueeze(2).to_broadcast([P, KW, D]), ALU.subtract))
    link(nc.vector.tensor_tensor(sq[:, :, :], xc[:, :, :], xc[:, :, :], ALU.mult))
    link(nc.vector.tensor_reduce(var, sq[:, :, :], AX.X, ALU.add))
    link(nc.vector.tensor_scalar(var, var, 1.0 / D, EPS, ALU.mult, ALU.add))


def layer_phase(nc, sem, layer, env):
    name = f"layer{layer}_"
    mlp = layer == 2
    final = layer == 3
    nxt = layer + 1
    acc = env["hidden_acc"] if mlp else env["acc"]
    table, next_table = env["tables"][layer], env["tables"][nxt]
    idx = env["idx_rel"] if layer == 0 else env["idx_src"]
    own_weights, sum_weights = env["own_weights"][nxt], env["sum_weights"][layer]
    wp2_deg, wp3b, w_edge = env["wp2_deg"], env["wp3b"], env["w_edge"]
    ident, ident_bf, iota, window_iota = env["ident"], env["ident_bf"], env["iota"], env["window_iota"]
    xs, rel_dst, edge_attr, out = env["xs"], env["rel_dst"], env["edge_attr"], env["out"]
    width = H if mlp else D
    sums = D + FE + 1 if layer == 0 else width

    idx_in = [sem(name + f"idx_in{g}") for g in range(PER)]
    gather_begun = sem(name + "gather_begun")
    branch_begun = sem(name + "branch_begun")
    gathered = [sem(name + f"gathered{g}") for g in range(PER)]
    sel_ready = sem(name + "sel_ready")
    summed = sem(name + "summed")
    acc_added = sem(name + "acc_added")
    cleared = sem(name + "cleared")
    shifted = sem(name + "shifted")
    if layer in (0, 2):
        attr_in = [sem(name + f"attr_in{g}") for g in range(PER)]
    if layer == 0:
        attr_ready = sem(name + "attr_ready")
    if mlp:
        rcv_in = [sem(name + f"rcv_in{g}") for g in range(PER)]
        flipped = sem(name + "flipped")
        flip_ready = sem(name + "flip_ready")
        pre_ready = sem(name + "pre_ready")
        pre_added = sem(name + "pre_added")
        relu_ready = sem(name + "relu_ready")
    SLOT_PER, SLOT, DONE = 1, 1 + PER - SLOTS, 1 + PER
    block_final = sem(name + "block_final")
    staged = sem(name + "staged")
    lin_ready = sem(name + "lin_ready")
    lin_copied = sem(name + "lin_copied")
    post_ready = sem(name + "post_ready")
    x_posted = sem(name + "x_posted")
    step = sem(name + "step")
    var_ready = sem(name + "var_ready")
    std_ready = sem(name + "std_ready")
    h_ready = sem(name + "h_ready")
    turn_begun = sem(name + "turn_begun")
    turned = sem(name + "turned")
    ht_ready = sem(name + "ht_ready")
    own_ready = sem(name + "own_ready")
    own_added = sem(name + "own_added")
    rows_ready = sem(name + "rows_ready")
    rows_copied = sem(name + "rows_copied")
    stored = sem(name + "stored")
    zero_ready = sem(name + "zero_ready")

    with ExitStack() as scope:
        def sb(n, shape, dt=F32):
            return scope.enter_context(nc.sbuf_tensor(name + n, shape, dt))

        def ps(n, shape=(P, 512), dt=F32):
            return scope.enter_context(nc.psum_tensor(name + n, list(shape), dt))

        idx_slot = [sb(f"idx{g}", [P, TILES], I32) for g in range(PER)]
        msg = [sb(f"msg{g}", [P, TILES, P if layer == 0 else width]) for g in range(PER)]
        sel = [sb(f"sel{j}", [P, TILES, P]) for j in range(SLOTS)]
        attr = [sb(f"attr{j}", [P, TILES * FE]) for j in range(SLOTS)] if layer in (0, 2) else None
        sum_ps = [ps(f"sum_ps{i}") for i in range(2)]
        if mlp:
            sel_bf = [sb(f"sel_bf{j}", [P, TILES, P], BF16) for j in range(SLOTS)]
            sel_t = [sb(f"sel_t{i}", [P, TILES * P]) for i in range(2)]
            attr_t = [sb(f"attr_t{i}", [P, P]) for i in range(2)]
            rcv = [sb(f"rcv{j}", [P, H]) for j in range(SLOTS)]
            flip_ps = ps("flip_ps")
            sel_ps = flip_ps[:, 0:TILES * P // 2].bitcast(BF16)
            attr_ps = flip_ps[:, TILES * P // 2:TILES * P // 2 + P]
            pre_ps = [ps(f"pre_ps{i}") for i in range(2)]
        stage_rows = {0: D, 1: D, 2: H, 3: D + FE + 1}[layer]
        stage = sb("stage", [P, BLK])
        stage_deg = sb("stage_deg", [P, BLK]) if mlp else None
        lin = sb("lin", [P, BLK]) if final else None
        mean = sb("mean", [P, KW])
        rstd = sb("rstd", [P, KW])
        deg = sb("deg", [P, KW, 1])
        xc = sb("xc", [P, KW, D])
        sq = sb("sq", [P, KW, D])
        h = sb("h", [P, KW, D])
        ht = sb("ht", [D + 1, BLK])
        rows = sb("rows", [P, 2, KW * H]) if nxt == 2 else None
        zero_rows = sb("zero_rows", [P, H]) if nxt == 2 else None
        post_ps = ps("post_ps")
        own_ps = ps("own_ps") if not final else None
        ht_ps = ps("ht_ps") if not final else None
        row_ps = [ps(f"row_ps{i}") for i in range(2)] if nxt == 2 else None
        lin_ps = ps("lin_ps", (P, 1024)) if final else None
        out_w = D + 1 if mlp else D
        stores = 2 if nxt == 2 else 1
        steps = (4 if mlp else 1) + (0 if final else 8)
        halves = [range(0, 4), range(4, KW)]
        out_blocks = out[0:(NB - 1) * BLK, :].rearrange("(b p k) f -> b p (k f)", p=P, k=KW)

        def load_passes(eng):
            return eng.value_load(env["passes"][0:1, 0:1], min_val=1, max_val=MAX_PASSES)

        def load_bases(engine_type, p, i):
            _, values = nc.values_load_multi_w_load_instructions(
                env["base_row"][0:1, bass.ds(i * PER, PER)], engines=[engine_type], min_val=0, max_val=N - 1)
            return [nc.s_assert_within(v + p * P, min_val=0, max_val=N - 1,
                                       skip_runtime_bounds_check_because="the table is zero where p is not")
                    for v in values]

        def run(eng, engine_type, edges, nodes, each_pass=None):
            n_passes = load_passes(eng)
            with eng.Fori(0, n_passes) as p:
                with eng.Fori(0, NB) as b:
                    _, (lo, hi) = nc.values_load_multi_w_load_instructions(
                        env["schedule"][0:1, bass.ds(b, 2)], engines=[engine_type], min_val=0, max_val=ITERS)
                    with eng.If(lo < hi):
                        with eng.Fori(lo, hi) as i:
                            edges(p, nc.s_assert_within(
                                i, min_val=0, max_val=ITERS - 1,
                                skip_runtime_bounds_check_because="the schedule ends at ITERS"))
                    with eng.If(p == n_passes - 1):
                        nodes(b)
                if each_pass:
                    each_pass(p)

        with nc.Block() as block:
            @block.gpsimd
            def _(pool):
                of = table[0] if mlp else table
                with pool.Fori(0, load_passes(pool)) as p:
                    with pool.Fori(0, ITERS) as i:
                        n = p * ITERS + i
                        for g in range(PER):
                            pool.wait_ge(idx_in[g], n * 16 + 16)
                            pool.wait_ge(summed, n * PER + g + SLOT_PER)
                            pool.sem_inc(gather_begun, 1)
                            for u in range(TILES):
                                nc.gpsimd.indirect_dma_start(
                                    msg[g][:, u, 0:width], None, of,
                                    bass.IndirectOffsetOnAxis(ap=idx_slot[g][:, u:u + 1], axis=0),
                                ).then_inc(gathered[g], 16)

            @block.sync
            def _(sp):
                full = E // GE
                tail_parts = (E - full * GE) // TILES
                groups = edge_attr[0:full * GE, :].rearrange("(g p u) f -> g p (u f)", p=P, u=TILES)

                def load_idx(i, g):
                    sp.dma_start(idx_slot[g][:, :],
                                 idx[:, bass.ds((i * PER + g) * TILES, TILES)]).then_inc(idx_in[g], 16)

                def load_attr(p, i, g, bases):
                    n, j = p * ITERS + i, g % SLOTS
                    sp.wait_ge(flipped if mlp else attr_ready, n * PER + g + 1)
                    if (ITERS - 1) * PER + g < full:
                        sp.dma_start(attr[j][:, :],
                                     groups[bass.ds(i * PER + g, 1)].rearrange("a p f -> (a p) f")
                                     ).then_inc(attr_in[g], 16)
                    else:
                        sp.sem_inc(branch_begun, 1)
                        with sp.If(i < ITERS - 1):
                            safe = nc.s_assert_within(
                                i * PER + g, min_val=0, max_val=full - 1,
                                skip_runtime_bounds_check_because="i is below the last iteration")
                            sp.dma_start(attr[j][:, :],
                                         groups[bass.ds(safe, 1)].rearrange("a p f -> (a p) f")
                                         ).then_inc(attr_in[g], 16)
                        with sp.Else():
                            if (ITERS - 1) * PER + g == full:
                                sp.dma_start(attr[j][0:tail_parts, :],
                                             edge_attr[full * GE:E, :].rearrange("(p u) f -> p (u f)",
                                                                                 u=TILES)
                                             ).then_inc(attr_in[g], 16)
                            else:
                                sp.dma_start(attr[j][:, :], groups[full - 1]).then_inc(attr_in[g], 16)
                    if mlp:
                        sp.wait_ge(pre_ready, n * PER + g + 1)
                        sp.dma_start(rcv[j][:, :],
                                     table[1][bass.ds(bases[g], P), :]).then_inc(rcv_in[g], 16)

                for g in range(PER):
                    load_idx(0, g)
                with sp.Fori(0, load_passes(sp)) as p:
                    with sp.Fori(0, ITERS) as i:
                        bases = load_bases(SP_ENGINE, p, i) if mlp else None
                        if attr is not None:
                            for g in range(SLOTS):
                                load_attr(p, i, g, bases)
                        for g in range(PER):
                            sp.wait_ge(gathered[g], (p * ITERS + i + 1) * TILES * 16)
                            load_idx(i + 1, g)
                            if attr is not None and g + SLOTS < PER:
                                load_attr(p, i, g + SLOTS, bases)
                n_passes = load_passes(sp)
                for g in range(PER):
                    sp.wait_ge(idx_in[g], n_passes * (ITERS * 16) + 16)
                sp.sem_inc(branch_begun, 1)

            @block.scalar
            def _(act):
                if mlp:
                    act.sem_inc(flip_ready, 1)
                act.sem_inc(stored, 16 * stores)
                if layer == 0:
                    act.sem_inc(attr_ready, SLOTS)
                    for g in range(PER):
                        nc.scalar.activation(msg[g][:, :, D + FE:D + FE + 1],
                                             ident[:, 0:TILES].unsqueeze(2), ACT.Copy, bias=1.0, scale=0.0)
                if not final:
                    act.sem_inc(ht_ready, 1)
                if nxt == 2:
                    act.sem_inc(rows_copied, 2)

                def place_attr(n, g):
                    j = g % SLOTS
                    act.wait_ge(attr_in[g], n * 16 + 16)
                    act.wait_ge(summed, n * PER + g + SLOT_PER)
                    nc.scalar.copy(msg[g][:, :, D:D + FE],
                                   attr[j][:, :].rearrange("p (u f) -> p u f", u=TILES)).then_inc(attr_ready, 1)

                def copy_flipped(n, g):
                    act.wait_ge(flipped, n * PER + g + 1 + SLOTS)
                    act.wait_ge(pre_ready, n * PER + g + 3)
                    nc.scalar.copy(attr_t[g % 2][:, :], attr_ps)
                    nc.scalar.copy(sel_t[g % 2][:, :], sel_ps).then_inc(flip_ready, 1)

                def relu(n, g):
                    act.wait_ge(pre_added, n * PER + g + DONE)
                    nc.scalar.activation(msg[g][:, :, :], msg[g][:, :, :], ACT.Relu).then_inc(relu_ready, 1)

                def edges(p, i):
                    n = p * ITERS + i
                    if layer == 0:
                        for g in range(PER):
                            place_attr(n, g)
                    if mlp:
                        for t in range(PER + 1):
                            if t < PER:
                                copy_flipped(n, t)
                            if t >= 1:
                                relu(n, t - 1)

                def nodes(b):
                    act.wait_ge(block_final, b + 1)
                    at = bass.ds(b * BLK, BLK)
                    if mlp:
                        nc.scalar.copy(stage_deg[D + FE:D + FE + 1, :], env["acc"][D + FE:D + FE + 1, at])
                    nc.scalar.copy(stage[0:stage_rows, :], acc[0:stage_rows, at]).then_inc(staged, 1)
                    if final:
                        act.wait_ge(lin_ready, b + 1)
                        half = BLK // 2
                        nc.scalar.copy(lin[:, :].rearrange("p (t c) -> p t c", t=2),
                                       lin_ps[:, :].rearrange("p (t c) -> p t c", t=2)[:, :, 0:half]
                                       ).then_inc(lin_copied, 1)
                        act.wait_ge(x_posted, b + 1)
                        act.sem_inc(branch_begun, 1)
                        with act.If(b < NB - 1):
                            safe = nc.s_assert_within(b, min_val=0, max_val=NB - 2,
                                                      skip_runtime_bounds_check_because="it is tested")
                            act.dma_start(out_blocks[bass.ds(safe, 1)].rearrange("a p f -> (a p) f"),
                                          xs[:, bass.ds(safe, 1), :].rearrange("p a f -> p (a f)")
                                          ).then_inc(stored, 16)
                        return
                    act.wait_ge(var_ready, b + 1)
                    nc.scalar.activation(rstd[:, :], rstd[:, :], ACT.Sqrt).then_inc(std_ready, 1)
                    if nxt != 2:
                        act.wait_ge(h_ready, b + 1)
                        to = next_table.rearrange("(b p k) f -> b p (k f)", p=P, k=KW)
                        act.dma_start(to[bass.ds(b, 1)].rearrange("a p f -> (a p) f"),
                                      h[:, :, :].rearrange("p k f -> p (k f)")).then_inc(stored, 16)
                    for t, windows in enumerate(halves):
                        w0, cols = windows[0] * P, len(windows) * P
                        act.wait_ge(turned, b * 2 + t + 1)
                        nc.scalar.copy(ht[0:D, w0:w0 + cols], ht_ps[0:D, 0:cols]).then_inc(ht_ready, 1)
                    if nxt == 2:
                        act.wait_ge(stored, 16 * stores * (b + 1))
                        for k in range(KW):
                            act.wait_ge(rows_ready, b * KW + k + 1)
                            nc.scalar.copy(rows[:, :, k * H:(k + 1) * H],
                                           row_ps[k % 2][:, 0:2 * H].rearrange("p (t f) -> p t f", t=2)
                                           ).then_inc(rows_copied, 1)
                        act.wait_ge(rows_copied, (b + 1) * KW + 2)
                        for t in range(2):
                            to = next_table[t][0:NPAD, :].rearrange("(b p k) f -> b p (k f)", p=P, k=KW)
                            act.dma_start(to[bass.ds(b, 1)].rearrange("a p f -> (a p) f"),
                                          rows[:, t, :]).then_inc(stored, 16)

                run(act, ACT_ENGINE, edges, nodes)
                total = NB * stores + stores
                if final:
                    n0 = (NB - 1) * BLK
                    tail_full = (N - n0) // KW
                    tail_nodes = N - n0 - tail_full * KW
                    act.dma_start(out[n0:n0 + tail_full * KW, :].rearrange("(p k) f -> p (k f)", k=KW),
                                  xs[0:tail_full, NB - 1, :]).then_inc(stored, 16)
                    act.dma_start(out[N - tail_nodes:N, :].rearrange("(a k) f -> a (k f)", a=1),
                                  xs[tail_full:tail_full + 1, NB - 1, 0:tail_nodes * D]).then_inc(stored, 16)
                    total += 1
                if nxt == 2:
                    act.wait_ge(zero_ready, 1)
                    act.dma_start(next_table[1][NPAD:ACC_W, :], zero_rows[:, :]).then_inc(stored, 16)
                    total += 1
                act.wait_ge(stored, 16 * total)

            @block.vector
            def _(dve):
                nc.vector.tensor_copy(window_iota[:, :], iota[:, :]).then_inc(shifted, 1)
                if layer == 0:
                    nc.vector.memset(stage[D:D + 1, :], 1.0)
                if not final:
                    nc.vector.memset(ht[D:D + 1, :], 1.0)
                if nxt == 2:
                    nc.vector.memset(zero_rows[:, :], 0.0).then_inc(zero_ready, 1)
                nc.vector.memset(acc[0:sums, :], 0.0).then_inc(cleared, 1)
                dve.sem_inc(acc_added, 2)
                if mlp:
                    dve.sem_inc(pre_added, PER)
                dve.wait_ge(shifted, 1)
                dve.wait_ge(cleared, 1)

                def select(n, i, g):
                    j = g % SLOTS
                    dve.wait_ge(summed, n * PER + g + SLOT)
                    rel = rel_dst[:, bass.ds((i * PER + g) * TILES, TILES)]
                    nc.vector.tensor_tensor(sel[j][:, :, :], rel.unsqueeze(2).to_broadcast([P, TILES, P]),
                                            window_iota[:, :].unsqueeze(1).to_broadcast([P, TILES, P]),
                                            ALU.is_equal).then_inc(sel_ready, 1)
                    if mlp:
                        dve.wait_ge(sel_ready, (n * PER + g) * 2 + 1)
                        nc.vector.tensor_copy(sel_bf[j][:, :, :], sel[j][:, :, :]).then_inc(sel_ready, 1)

                def add_sender(n, g):
                    dve.wait_ge(pre_ready, n * PER + g + 1 + SLOTS)
                    dve.wait_ge(gathered[g], (n + 1) * TILES * 16)
                    rows_of = msg[g][:, :, :].rearrange("p u f -> p (u f)")
                    nc.vector.tensor_tensor(rows_of, pre_ps[g % 2][:, :], rows_of, ALU.add).then_inc(pre_added, 1)

                def add_sums(n, g, base):
                    dve.wait_ge(summed, n * PER + g + DONE)
                    dve.wait_ge(acc_added, n * PER + g + 2)
                    to = acc[0:sums, bass.ds(base, P)]
                    nc.vector.tensor_tensor(to, to, sum_ps[g % 2][0:sums, 0:P], ALU.add).then_inc(acc_added, 1)

                def edges(p, i):
                    n = p * ITERS + i
                    bases = load_bases(DVE_ENGINE, p, i)
                    select(n, i, 0)
                    for t in range(PER + (2 if mlp else 0)):
                        if t + 1 < PER:
                            select(n, i, t + 1)
                        if mlp and 1 <= t <= PER:
                            add_sender(n, t - 1)
                        if not mlp:
                            add_sums(n, t, bases[t])
                        elif t >= 2:
                            add_sums(n, t - 2, bases[t - 2])
                    dve.wait_ge(acc_added, (n + 1) * PER + 2)

                def nodes(b):
                    dve.sem_inc(block_final, 1)
                    xb = xs[:, bass.ds(b, 1), :].rearrange("p a (k f) -> p (a k) f", k=KW)
                    done = [0]

                    def link(ins):
                        done[0] += 1
                        ins.then_inc(step, 1)
                        dve.wait_ge(step, b * steps + done[0])

                    dve.wait_ge(post_ready, b + 1)
                    add = post_ps[:, 0:KW * out_w].rearrange("p (k f) -> p k f", f=out_w)
                    if mlp:
                        link(nc.vector.tensor_scalar(deg[:, :, :], add[:, :, D:D + 1], 1.0, None, ALU.max))
                        link(nc.vector.reciprocal(deg[:, :, :], deg[:, :, :]))
                        link(nc.vector.tensor_tensor(sq[:, :, :], add[:, :, 0:D],
                                                     deg[:, :, :].to_broadcast([P, KW, D]), ALU.mult))
                        add = sq[:, :, :]
                    link(nc.vector.tensor_tensor(xb, xb, add[:, :, 0:D], ALU.add))
                    dve.sem_inc(x_posted, 1)
                    if final:
                        return
                    norm_steps(nc, link, xb, mean[:, :], rstd[:, :], xc, sq)
                    dve.sem_inc(var_ready, 1)
                    dve.wait_ge(std_ready, b + 1)
                    link(nc.vector.reciprocal(rstd[:, :], rstd[:, :]))
                    if nxt != 2:
                        dve.wait_ge(stored, 16 * (b + 1))
                    nc.vector.scalar_tensor_tensor(
                        out=h[:, :, :], in0=xc[:, :, :], scalar=0.0,
                        in1=rstd[:, :].unsqueeze(2).to_broadcast([P, KW, D]), op0=ALU.max,
                        op1=ALU.mult).then_inc(h_ready, 1)
                    dve.wait_ge(own_ready, b + 1)
                    link(nc.vector.tensor_tensor(xb, xb, own_ps[:, 0:KW * D].rearrange(
                        "p (k f) -> p k f", k=KW), ALU.add))
                    dve.sem_inc(own_added, 1)

                def next_window(p):
                    nc.vector.tensor_scalar(window_iota[:, :], window_iota[:, :], float(P), None,
                                            ALU.add).then_inc(shifted, 1)
                    dve.wait_ge(shifted, p + 2)

                run(dve, DVE_ENGINE, edges, nodes, next_window)

            @block.tensor
            def _(pe):
                pe.sem_inc(summed, PER)
                if mlp:
                    pe.sem_inc(flipped, SLOTS)
                    pe.sem_inc(pre_ready, SLOTS)

                def flip(n, g):
                    j = g % SLOTS
                    pe.wait_ge(sel_ready, (n * PER + g) * 2 + 2)
                    pe.wait_ge(attr_in[g], n * 16 + 16)
                    pe.wait_ge(flip_ready, n * PER + g + 1)
                    for u in range(TILES):
                        nc.tensor.transpose(sel_ps[:, u * P:(u + 1) * P], sel_bf[j][:, u, :], ident_bf[:, :])
                    nc.tensor.transpose(attr_ps, attr[j][:, :], ident[:, :]).then_inc(flipped, 1)

                def hidden(n, g):
                    j = g % SLOTS
                    pe.wait_ge(flip_ready, n * PER + g + 2)
                    pe.wait_ge(rcv_in[g], n * 16 + 16)
                    pe.wait_ge(pre_added, n * PER + g + DONE - 2)
                    nc.tensor.matmul(pre_ps[g % 2][:, :], attr_t[g % 2][:, :], w_edge[:, :], start=True,
                                     stop=False)
                    for u in range(TILES):
                        last = nc.tensor.matmul(pre_ps[g % 2][:, u * H:(u + 1) * H],
                                                sel_t[g % 2][:, u * P:(u + 1) * P], rcv[j][:, :],
                                                start=False, stop=u == TILES - 1)
                    last.then_inc(pre_ready, 1)

                def sum_up(n, g):
                    j = g % SLOTS
                    pe.wait_ge(acc_added, n * PER + g + 1)
                    if mlp:
                        pe.wait_ge(relu_ready, n * PER + g + 1)
                    else:
                        pe.wait_ge(sel_ready, n * PER + g + 1)
                        pe.wait_ge(gathered[g], (n + 1) * TILES * 16)
                    if layer == 0:
                        pe.wait_ge(attr_ready, n * PER + g + 1 + SLOTS)
                    for u in range(TILES):
                        lhs = msg[g][:, u, 0:sums]
                        last = nc.tensor.matmul(sum_ps[g % 2][0:sums, 0:P], lhs, sel[j][:, u, :], start=u == 0,
                                                stop=u == TILES - 1)
                    last.then_inc(summed, 1)

                def edges(p, i):
                    n = p * ITERS + i
                    for t in range(PER + (2 if mlp else 0)):
                        if not mlp:
                            sum_up(n, t)
                            continue
                        if t < PER:
                            flip(n, t)
                        if 1 <= t <= PER:
                            hidden(n, t - 1)
                        if t >= 2:
                            sum_up(n, t - 2)

                def nodes(b):
                    sums_at, weights, k_rows = stage, sum_weights, D + 1 if layer == 0 else stage_rows
                    pe.wait_ge(staged, b + 1)
                    if final:
                        half = BLK // 2
                        for t in range(2):
                            last = nc.tensor.matmul(lin_ps[:, t * 512:t * 512 + half], weights[0:k_rows, :],
                                                    stage[0:k_rows, t * half:(t + 1) * half], start=True,
                                                    stop=True)
                        last.then_inc(lin_ready, 1)
                        pe.wait_ge(lin_copied, b + 1)
                        sums_at, weights, k_rows = lin, wp3b, H
                    for k in range(KW):
                        to, windows = post_ps[:, k * out_w:(k + 1) * out_w], slice(k, BLK, KW)
                        last = nc.tensor.matmul(to, sums_at[0:k_rows, windows], weights[0:k_rows, 0:out_w],
                                                start=True, stop=not mlp)
                        if mlp:
                            last = nc.tensor.matmul(to, stage_deg[D + FE:D + FE + 1, windows],
                                                    wp2_deg[D + FE:D + FE + 1, :], start=False, stop=True)
                    last.then_inc(post_ready, 1)
                    if final:
                        return
                    pe.wait_ge(h_ready, b + 1)
                    for t, windows in enumerate(halves):
                        pe.wait_ge(ht_ready, b * 2 + t + 1)
                        pe.sem_inc(turn_begun, 1)
                        for k in windows:
                            at = (k - windows[0]) * P
                            last = nc.tensor.transpose(ht_ps[0:D, at:at + P], h[:, k, :], ident[:, :])
                        last.then_inc(turned, 1)
                    pe.wait_ge(ht_ready, b * 2 + 3)
                    for k in range(KW):
                        last = nc.tensor.matmul(own_ps[:, k * D:(k + 1) * D], ht[:, k * P:(k + 1) * P],
                                                own_weights[:, 0:D], start=True, stop=True)
                    last.then_inc(own_ready, 1)
                    if nxt != 2:
                        return
                    for k in range(KW):
                        pe.wait_ge(rows_copied, b * KW + k + (2 if k == 0 else 1))
                        nc.tensor.matmul(row_ps[k % 2][:, 0:2 * H],
                                         ht[:, k * P:(k + 1) * P], own_weights[:, D:D + 2 * H],
                                         start=True, stop=True).then_inc(rows_ready, 1)

                run(pe, PE_ENGINE, edges, nodes)


_INS = ["x", "src", "dst", "edge_attr_32", "edge_type_16", "L0_gnn_weight", "L0_gnn_h_bias",
        "L0_gnn_loop_weight", "L1_gnn_W", "L1_gnn_b", "L2_gnn_W1", "L2_gnn_b1", "L2_gnn_W2", "L2_gnn_b2",
        "L2_gnn_Wn", "L2_gnn_bn", "L3_gnn_W1", "L3_gnn_b1", "L3_gnn_W2", "L3_gnn_b2"]


def kernel(**inputs):
    import numpy as _np
    import concourse.bacc as _bacc
    from concourse import mybir as _mybir
    from concourse.bass_utils import run_bass_kernel_spmd as _run

    nc = _bacc.Bacc("TRN2", target_bir_lowering=False, num_devices=1)
    arrays, args = {}, []
    for name in _INS:
        a = _np.ascontiguousarray(inputs[name])
        arrays[f"in_{name}_dram"] = a
        args.append(nc.dram_tensor(f"in_{name}_dram", a.shape, _mybir.dt.from_np(a.dtype),
                                   kind="ExternalInput").ap())
    out = nc.dram_tensor("out_0_dram", (N, D), _mybir.dt.float32, kind="ExternalOutput").ap()
    gnn_program(nc, *args, out)
    r = _run(nc, [arrays], core_ids=[0])
    return r.results[0]["out_0_dram"]
```

```python
from contextlib import ExitStack

import concourse.bass as bass
from concourse import mybir

F32 = mybir.dt.float32
BF16 = mybir.dt.bfloat16
I32 = mybir.dt.int32
ALU = mybir.AluOpType
ACT = mybir.ActivationFunctionType
AX = mybir.AxisListType
DVE_ENGINE = mybir.EngineType.DVE
SP_ENGINE = mybir.EngineType.SP
ACT_ENGINE = mybir.EngineType.Activation
PE_ENGINE = mybir.EngineType.PE

P = 128
D = 64
FE = 32
H = 128
RELS = 16
DEG = D + FE
N = 12500
E = 200000

KW = 7
BLK = P * KW
NB = -(-N // BLK)
NPAD = NB * BLK
ACC_W = NPAD + P
PAIRS = NB // 2

TILES = 4
GE = P * TILES
PER = 8
SLOTS = 4
ITERS = -(-E // (GE * PER))
G = ITERS * PER
CH = -(-G // P)
PAD_DST = -1000000.0
MAX_PASSES = -(-N // P)
EPS = 1e-5

assert NB % 2 == 0 and GE == 512


def gnn_program(nc, x, src, dst, edge_attr, edge_type, w_rel, b_rel, w_loop, w_sum, b_sum,
                w1_mlp, b1_mlp, w2_mlp, b2_mlp, wn_mlp, bn_mlp, w1_lin, b1_lin, w2_lin, b2_lin, out):
    rel_table = nc.dram_tensor("rel_table", [NPAD * RELS, D], F32).ap()
    h1_table = nc.dram_tensor("h1_table", [NPAD, D], F32).ap()
    snd_table = nc.dram_tensor("snd_table", [NPAD, H], F32).ap()
    rcv_table = nc.dram_tensor("rcv_table", [ACC_W, H], F32).ap()
    h3_table = nc.dram_tensor("h3_table", [NPAD, D], F32).ap()

    with ExitStack() as ctx:
        def sb(name, shape, dt=F32, scope=ctx):
            return scope.enter_context(nc.sbuf_tensor(name, shape, dt))

        held = []

        def sem(name):
            held.append(nc.alloc_semaphore(name=name))
            return held[-1]

        def end_phase():
            nc.clear_and_free_semaphores(held)
            held.clear()
            nc.all_engine_barrier()

        xs = sb("xs", [P, NB, KW * D])
        acc = sb("acc", [P, ACC_W])
        rel_dst = sb("rel_dst", [P, (G + PER) * TILES])
        idx_src = sb("idx_src", [P, (G + PER) * TILES], I32)
        idx_rel = sb("idx_rel", [P, (G + PER) * TILES], I32)
        base_row = sb("base_row", [1, CH * P], I32)
        schedule = sb("schedule", [1, NB + 1], I32)
        passes = sb("passes", [1, 1], I32)
        share = sb("share", [P, NB, KW])
        iota = sb("iota", [P, P])
        ident = sb("ident", [P, P])
        ident_bf = sb("ident_bf", [P, P], BF16)
        wc1 = sb("wc1", [D + 1, D])
        wc2 = sb("wc2", [DEG + 1, D + 2 * H])
        wc3 = sb("wc3", [D + 1, D])
        wp0 = sb("wp0", [D + 1, D])
        wp1 = sb("wp1", [DEG + 1, D + 1])
        wp2 = sb("wp2", [H, D])
        wp3a = sb("wp3a", [D + FE + 1, H])
        wp3b = sb("wp3b", [H, D])
        w_edge = sb("w_edge", [P, TILES * H])

        with ExitStack() as early:
            w0_parts = sb("w0_parts", [P, 3, D + RELS * D], BF16, early)
            setup(nc, sem, locals())
            end_phase()
            first_nodes(nc, sem, xs, w0_parts, rel_table, ident)
            end_phase()
        hidden_acc = sb("hidden_acc", [P, ACC_W])

        env = locals()
        env["own_weights"] = [None, wc1, wc2, wc3, None]
        env["sum_weights"] = [wp0, wp1, wp2, wp3a]
        env["tables"] = [rel_table, h1_table, (snd_table, rcv_table), h3_table, None]
        for layer in range(4):
            layer_phase(nc, sem, layer, env)
            if layer < 3:
                end_phase()


def setup(nc, sem, env):
    x, src, dst, edge_type = env["x"], env["src"], env["dst"], env["edge_type"]
    xs, ident, iota, ident_bf = env["xs"], env["ident"], env["iota"], env["ident_bf"]
    wc1, wc2, wc3, wp0, w0_parts = env["wc1"], env["wc2"], env["wc3"], env["wp0"], env["w0_parts"]
    schedule = env["schedule"]
    wp1, wp2, wp3a, wp3b = env["wp1"], env["wp2"], env["wp3a"], env["wp3b"]
    w_edge, acc, base_row, passes = env["w_edge"], env["acc"], env["base_row"], env["passes"]

    zeroed = sem("setup_zeroed")
    const_ready = sem("setup_const_ready")
    edges_loaded = sem("setup_edges_loaded")
    loaded = sem("setup_loaded")
    everything = sem("setup_everything")
    chain = sem("setup_chain")
    bad_ready = sem("setup_bad_ready")
    bad_summed = sem("setup_bad_summed")
    lists_ready = sem("setup_lists_ready")
    ready_made = sem("setup_ready_made")
    turned = sem("setup_turned")
    evacuated = sem("setup_evacuated")

    with ExitStack() as scope:
        def sb(name, shape, dt=F32):
            return scope.enter_context(nc.sbuf_tensor(name, shape, dt))

        raw_dst = sb("raw_dst", [P, CH, GE], I32)
        raw_src = sb("raw_src", [P, CH, GE], I32)
        raw_typ = sb("raw_typ", [P, CH, GE], I32)
        dst_f = sb("dst_f", [P, CH, GE])
        src_f = sb("src_f", [P, CH, GE])
        row_f = sb("row_f", [P, CH, GE])
        off_f = sb("off_f", [P, CH, GE])
        real = sb("real", [P, CH, GE])
        bad = sb("bad", [P, CH, GE])
        first = sb("first", [P, CH])
        base_f = sb("base_f", [P, CH])
        any_bad = sb("any_bad", [P, 1])
        fast = sb("fast", [P, 1])
        ones = sb("ones", [P, P])
        part = sb("part", [P, 1])
        w_sum_raw = sb("w_sum_raw", [D, 2 * D])
        w0 = sb("w0", [P, D + RELS * D])
        base_wide = sb("base_wide", [P, CH, NB])
        block_end = sb("block_end", [P, 1])
        iteration = sb("iteration", [NB, G])
        touched = sb("touched", [NB, G])
        ready = sb("ready", [NB, 1])
        turn_ps = [scope.enter_context(nc.psum_tensor(f"turn_ps{i}", [P, 512], F32)) for i in range(4)]
        row_ps = scope.enter_context(nc.psum_tensor("row_ps", [P, 512], F32))
        sum_ps = scope.enter_context(nc.psum_tensor("sum_ps", [P, 512], F32))
        w_ps = scope.enter_context(nc.psum_tensor("w_ps", [P, 512], F32))

        full_rows = E // (P * GE) * P * GE
        tail_rows = (E - full_rows) // GE
        tail_edges = E - full_rows - tail_rows * GE
        full_blocks = N // BLK
        tail_parts = (N - full_blocks * BLK) // KW
        tail_nodes = N - full_blocks * BLK - tail_parts * KW
        lists = [(env["idx_src"], src_f), (env["idx_rel"], row_f), (env["rel_dst"], off_f)]

        with nc.Block() as block:
            @block.gpsimd
            def _(pool):
                nc.gpsimd.memset(raw_dst[:, CH - 1, :], int(PAD_DST)).then_inc(zeroed, 1)
                nc.gpsimd.memset(raw_src[:, CH - 1, :], 0).then_inc(zeroed, 1)
                nc.gpsimd.memset(raw_typ[:, CH - 1, :], 0).then_inc(zeroed, 1)
                nc.gpsimd.memset(xs[:, NB - 1, :], 0.0).then_inc(zeroed, 1)
                nc.gpsimd.memset(w_edge[:, :], 0.0).then_inc(zeroed, 1)
                nc.gpsimd.memset(wc2[:, :], 0.0).then_inc(zeroed, 1)
                nc.gpsimd.memset(wp1[:, :], 0.0).then_inc(zeroed, 1)
                nc.gpsimd.iota(iota[:, :], [[1, P]], base=0, channel_multiplier=0,
                               allow_small_or_imprecise_dtypes=True).then_inc(const_ready, 1)
                nc.gpsimd.iota(part[:, :], [[0, 1]], base=0, channel_multiplier=1,
                               allow_small_or_imprecise_dtypes=True).then_inc(const_ready, 1)
                nc.gpsimd.iota(block_end[:, :], [[0, 1]], base=BLK, channel_multiplier=BLK,
                               allow_small_or_imprecise_dtypes=True).then_inc(const_ready, 1)
                nc.gpsimd.iota(iteration[:, :].rearrange("b (i g) -> b i g", g=PER), [[1, ITERS], [0, PER]],
                               base=1, channel_multiplier=0,
                               allow_small_or_imprecise_dtypes=True).then_inc(const_ready, 1)
                nc.gpsimd.memset(ones[:, :], 1.0).then_inc(const_ready, 1)

            @block.sync
            def _(sp):
                edge_lists = ((raw_dst, dst), (raw_src, src), (raw_typ, edge_type))
                for raw, edges in edge_lists:
                    sp.dma_start(raw[:, 0:CH - 1, :],
                                 edges[0:full_rows].rearrange("(c g e) -> g c e", g=P, e=GE)
                                 ).then_inc(edges_loaded, 16)
                sp.wait_ge(zeroed, 3)
                for raw, edges in edge_lists:
                    sp.dma_start(raw[0:tail_rows, CH - 1, :],
                                 edges[full_rows:full_rows + tail_rows * GE].rearrange("(g e) -> g e", e=GE)
                                 ).then_inc(edges_loaded, 16)
                    sp.dma_start(raw[tail_rows:tail_rows + 1, CH - 1, 0:tail_edges],
                                 edges[E - tail_edges:E].rearrange("(a e) -> a e", a=1)
                                 ).then_inc(edges_loaded, 16)
                sp.wait_ge(zeroed, 7)
                loads = []
                n0 = full_blocks * BLK
                loads.append((xs[:, 0:full_blocks, :],
                              x[0:n0, :].rearrange("(b p k) f -> p b (k f)", p=P, k=KW)))
                loads.append((xs[0:tail_parts, full_blocks, :],
                              x[n0:n0 + tail_parts * KW, :].rearrange("(p k) f -> p (k f)", k=KW)))
                loads.append((xs[tail_parts:tail_parts + 1, full_blocks, 0:tail_nodes * D],
                              x[N - tail_nodes:N, :].rearrange("(a k) f -> a (k f)", a=1)))
                bias = lambda b: b.rearrange("(a f) -> a f", a=1)
                for half in range(2):
                    rows = w0[half * D:(half + 1) * D, :]
                    loads.append((rows[:, 0:D], env["w_loop"]))
                    loads.append((rows[:, D:].rearrange("i (r o) -> i r o", r=RELS),
                                  env["w_rel"].rearrange("r i o -> i r o")))
                loads.append((wp0[D:D + 1, 0:D], bias(env["b_rel"])))
                loads.append((w_sum_raw[:, :], env["w_sum"]))
                loads.append((wc1[D:D + 1, :], bias(env["b_sum"])))
                loads.append((wc2[0:D, 0:D], env["wn_mlp"]))
                loads.append((wc2[0:D, D:D + H], env["w1_mlp"][0:D, :]))
                loads.append((wc2[0:D, D + H:], env["w1_mlp"][D:2 * D, :]))
                loads.append((wc2[D:D + 1, 0:D], bias(env["bn_mlp"])))
                loads.append((wc2[D:D + 1, D + H:], bias(env["b1_mlp"])))
                for u in range(TILES):
                    loads.append((w_edge[FE * u:FE * u + FE, H * u:H * u + H], env["w1_mlp"][2 * D:, :]))
                loads.append((wp2[:, :], env["w2_mlp"]))
                loads.append((wc2[DEG:DEG + 1, 0:D], bias(env["b2_mlp"])))
                loads.append((wc3[0:D, :], env["w2_lin"][0:D, :]))
                loads.append((wc3[D:D + 1, :], bias(env["b2_lin"])))
                loads.append((wp3a[0:D + FE, :], env["w1_lin"]))
                loads.append((wp3a[D + FE:D + FE + 1, :], bias(env["b1_lin"])))
                loads.append((wp3b[:, :], env["w2_lin"][D:, :]))
                for to, of in loads:
                    sp.dma_start(to, of).then_inc(loaded, 16)
                sp.wait_ge(loaded, 16 * len(loads))
                sp.sem_inc(everything, 1)

            @block.vector
            def _(dve):
                done = [0]

                def link(ins):
                    done[0] += 1
                    ins.then_inc(chain, 1)
                    dve.wait_ge(chain, done[0])

                dve.wait_ge(const_ready, 5)
                link(nc.vector.tensor_scalar(ident[:, :], iota[:, :], part[:, 0:1], None, ALU.is_equal))
                link(nc.vector.tensor_copy(ident_bf[:, :], ident[:, :]))
                dve.wait_ge(edges_loaded, 9 * 16)
                link(nc.vector.tensor_copy(dst_f[:, :, :], raw_dst[:, :, :]))
                link(nc.vector.tensor_scalar(base_f[:, :], dst_f[:, :, 0], 0.0, float(N - 1), ALU.is_lt,
                                             ALU.mult))
                link(nc.vector.scalar_tensor_tensor(out=first[:, :], in0=dst_f[:, :, 0], scalar=0.0,
                                                    in1=base_f[:, :], op0=ALU.max, op1=ALU.add))

                def spread(t):
                    return t[:, :].unsqueeze(2).to_broadcast([P, CH, GE])

                nc.vector.tensor_scalar(real[:, :, :], dst_f[:, :, :], 0.0, None, ALU.is_ge)
                link(nc.vector.tensor_tensor(off_f[:, :, :], dst_f[:, :, :], spread(first), ALU.subtract))
                dve.wait_ge(lists_ready, 2)
                nc.vector.scalar_tensor_tensor(out=row_f[:, :, :], in0=src_f[:, :, :], scalar=float(RELS),
                                               in1=row_f[:, :, :], op0=ALU.mult,
                                               op1=ALU.add).then_inc(lists_ready, 1)
                link(nc.vector.scalar_tensor_tensor(out=real[:, :, :], in0=off_f[:, :, :], scalar=0.0,
                                                    in1=real[:, :, :], op0=ALU.is_lt, op1=ALU.mult))
                link(nc.vector.scalar_tensor_tensor(out=bad[:, :, :], in0=off_f[:, :, :], scalar=float(P),
                                                    in1=real[:, :, :], op0=ALU.is_ge, op1=ALU.add))
                nc.vector.tensor_reduce(any_bad[:, :], bad[:, :, :], AX.XY, ALU.max).then_inc(bad_ready, 1)
                dve.wait_ge(bad_summed, 1)
                link(nc.vector.tensor_scalar(fast[:, :], sum_ps[:, 0:1], 0.0, None, ALU.is_equal))
                nc.vector.tensor_scalar(passes[:, :], fast[0:1, :], float(1 - MAX_PASSES), float(MAX_PASSES),
                                        ALU.mult, ALU.add)
                link(nc.vector.tensor_scalar(base_f[:, :], first[:, :], fast[:, 0:1], None, ALU.mult))
                link(nc.vector.tensor_copy(base_wide[:, :, :],
                                           base_f[:, :].unsqueeze(2).to_broadcast([P, CH, NB])))
                nc.vector.tensor_tensor(off_f[:, :, :], dst_f[:, :, :], spread(base_f),
                                        ALU.subtract).then_inc(lists_ready, 1)
                dve.wait_ge(everything, 1)
                link(nc.vector.tensor_copy(w0_parts[:, 0, :], w0[:, :]))
                link(nc.vector.tensor_tensor(w0[:, :], w0[:, :], w0_parts[:, 0, :], ALU.subtract))
                link(nc.vector.tensor_copy(w0_parts[:, 1, :], w0[:, :]))
                nc.vector.tensor_tensor(w0_parts[0:D, 2, :], w0[0:D, :], w0_parts[0:D, 1, :], ALU.subtract)
                nc.vector.tensor_copy(w0_parts[D:P, 2, :], w0_parts[D:P, 0, :])
                nc.vector.tensor_copy(wp0[0:D, :], ident[0:D, 0:D])
                dve.wait_ge(turned, len(lists) * CH + 1)
                link(nc.vector.tensor_copy(base_row[:, :], row_ps[0:1, 0:CH * P]))
                nc.vector.memset(base_row[:, G:G + PER], P)
                link(nc.vector.scalar_tensor_tensor(out=touched[:, :], in0=row_ps[0:NB, 0:G],
                                                    scalar=block_end[0:NB, 0:1], in1=iteration[:, :],
                                                    op0=ALU.is_lt, op1=ALU.mult))
                nc.vector.tensor_reduce(ready[:, :], touched[:, :], AX.X, ALU.max).then_inc(ready_made, 1)
                dve.wait_ge(turned, len(lists) * CH + 3)
                nc.vector.tensor_copy(wc1[0:D, :], w_ps[0:D, 0:D])
                nc.vector.tensor_copy(wp1[0:D, 0:D], w_ps[0:D, D:2 * D])
                nc.vector.memset(wp1[DEG:DEG + 1, D:D + 1], 1.0)
                nc.vector.memset(schedule[:, 0:1], 0)
                dve.wait_ge(turned, len(lists) * CH + 4)
                nc.vector.tensor_copy(schedule[:, 1:NB + 1], sum_ps[0:1, 64:64 + NB])

            @block.tensor
            def _(pe):
                pe.wait_ge(chain, 1)
                for a, (_, laid) in enumerate(lists):
                    if a == 2:
                        pe.wait_ge(bad_ready, 1)
                        nc.tensor.matmul(sum_ps[:, 0:1], ones[:, :], any_bad[:, :], start=True,
                                         stop=True).then_inc(bad_summed, 1)
                    pe.wait_ge(lists_ready, (1, 3, 4)[a])
                    for c in range(CH):
                        n = a * CH + c
                        if n >= 4:
                            pe.wait_ge(evacuated, n - 3)
                        view = laid[:, c, :].rearrange("g (p u) -> g u p", u=TILES)
                        for u in range(TILES):
                            last = nc.tensor.transpose(turn_ps[n % 4][:, u * P:(u + 1) * P], view[:, u, :],
                                                       ident[:, :])
                        last.then_inc(turned, 1)
                for c in range(CH):
                    last = nc.tensor.matmul(row_ps[0:NB, c * P:(c + 1) * P], base_wide[:, c, :], ident[:, :],
                                            start=True, stop=True)
                last.then_inc(turned, 1)
                pe.wait_ge(everything, 1)
                for half in range(2):
                    nc.tensor.transpose(w_ps[0:D, half * D:(half + 1) * D],
                                        w_sum_raw[:, half * D:(half + 1) * D],
                                        ident[0:D, 0:D]).then_inc(turned, 1)
                pe.wait_ge(ready_made, 1)
                nc.tensor.matmul(sum_ps[0:1, 64:64 + NB], ready[:, :], ident[0:NB, 0:NB], start=True,
                                 stop=True).then_inc(turned, 1)

            @block.scalar
            def _(act):
                act.wait_ge(edges_loaded, 9 * 16)
                nc.scalar.copy(src_f[:, :, :], raw_src[:, :, :]).then_inc(lists_ready, 1)
                nc.scalar.copy(row_f[:, :, :], raw_typ[:, :, :]).then_inc(lists_ready, 1)
                for n in range(len(lists) * CH):
                    to, c = lists[n // CH][0], n % CH
                    groups = min(P, G - c * P)
                    act.wait_ge(turned, n + 1)
                    turned_lists = turn_ps[n % 4][:, :].rearrange("p (u g) -> p u g", u=TILES)
                    if c == 0:
                        nc.scalar.activation(
                            to[:, G * TILES:(G + PER) * TILES].rearrange("p (g u) -> p u g", u=TILES),
                            turned_lists[:, :, 0:PER], ACT.Copy,
                            bias=float(-P) if to is env["rel_dst"] else 0.0)
                    nc.scalar.copy(
                        to[:, c * GE:c * GE + groups * TILES].rearrange("p (g u) -> p u g", u=TILES),
                        turned_lists[:, :, 0:groups]).then_inc(evacuated, 1)


def first_nodes(nc, sem, xs, w0_parts, table, ident):
    step = sem("first_step")
    var_ready = sem("first_var_ready")
    std_ready = sem("first_std_ready")
    h_ready = sem("first_h_ready")
    turn_begun = sem("first_turn_begun")
    turned = sem("first_turned")
    high_ready = sem("first_high_ready")
    copy_begun = sem("first_copy_begun")
    high_copied = sem("first_high_copied")
    low_ready = sem("first_low_ready")
    own_ready = sem("first_own_ready")
    own_added = sem("first_own_added")
    rows_ready = sem("first_rows_ready")
    rows_copied = sem("first_rows_copied")
    stored = [sem(f"first_stored{k}") for k in range(KW)]
    STEPS = 11
    NORM_STEPS = 8

    with ExitStack() as scope:
        def sb(n, shape, dt=F32):
            return scope.enter_context(nc.sbuf_tensor("first_" + n, shape, dt))

        def ps(n, shape):
            return scope.enter_context(nc.psum_tensor("first_" + n, shape, F32))

        mean = sb("mean", [P, KW])
        rstd = sb("rstd", [P, KW])
        xc = sb("xc", [P, KW, D])
        sq = sb("sq", [P, KW, D])
        h = [sb(f"h{i}", [P, KW, D]) for i in range(2)]
        ht_ab = [sb(f"ht_ab{i}", [P, BLK], BF16) for i in range(2)]
        ht_ac = [sb(f"ht_ac{i}", [P, BLK], BF16) for i in range(2)]
        rest = sb("rest", [P, BLK])
        rows = [sb(f"rows{k}", [P, RELS * D]) for k in range(KW)]
        own_ps = ps("own_ps", [P, 512])
        ht_ps = ps("ht_ps", [P, 1024])
        row_ps = [ps(f"row_ps{i}", [P, 1024]) for i in range(2)]

        with nc.Block() as block:
            @block.tensor
            def _(pe):
                pe.sem_inc(turned, 2)
                pe.sem_inc(own_ready, 1)
                pe.sem_inc(rows_ready, 2 * KW)

                def turn(b, s):
                    pe.wait_ge(h_ready, b + 1)
                    pe.wait_ge(low_ready, b + 1)
                    pe.sem_inc(turn_begun, 1)
                    for k in range(KW):
                        last = nc.tensor.transpose(ht_ps[0:D, k * P:(k + 1) * P], h[s][:, k, :], ident[:, :])
                    last.then_inc(turned, 1)

                def products(b, s, more):
                    def project(to, k, c0, c1):
                        nodes = slice(k * P, (k + 1) * P)
                        nc.tensor.matmul(to, ht_ab[s][:, nodes], w0_parts[:, 0, c0:c1], start=True,
                                         stop=False)
                        nc.tensor.matmul(to, ht_ab[s][:, nodes], w0_parts[:, 1, c0:c1], start=False,
                                         stop=False)
                        return nc.tensor.matmul(to, ht_ac[s][:, nodes], w0_parts[:, 2, c0:c1],
                                                start=False, stop=True)

                    pe.wait_ge(low_ready, b + 2)
                    pe.wait_ge(high_copied, b + 1)
                    pe.wait_ge(own_added, b + 1)
                    for k in range(KW):
                        last = project(own_ps[:, k * D:(k + 1) * D], k, 0, D)
                    last.then_inc(own_ready, 1)
                    for k in range(KW):
                        if k == 3 and more:
                            turn(b + 1, 1 - s)
                        slot = (s * KW + k) % 2
                        pe.wait_ge(rows_copied, b * KW + k + 1)
                        for c in range(0, RELS * D, 512):
                            last = project(row_ps[slot][:, c:c + 512], k, D + c, D + c + 512)
                        last.then_inc(rows_ready, 1)

                turn(0, 0)
                with pe.Fori(0, PAIRS - 1) as q:
                    for s in range(2):
                        products(q * 2 + s, s, True)
                products(NB - 2, 0, True)
                products(NB - 1, 1, False)

            @block.scalar
            def _(act):
                act.sem_inc(rows_copied, 2)

                def root(b):
                    act.wait_ge(var_ready, b + 1)
                    nc.scalar.activation(rstd[:, :], rstd[:, :], ACT.Sqrt).then_inc(std_ready, 1)

                def first_part(b, s):
                    act.wait_ge(rows_ready, (b + 1) * KW)
                    act.wait_ge(turned, b + 3)
                    nc.scalar.copy(ht_ab[s][0:D, :], ht_ps[0:D, 0:BLK]).then_inc(high_ready, 1)

                def copy_rows(b, s, more):
                    for k in range(KW):
                        if k == 1 and more:
                            root(b + 1)
                        if k == 3 and more:
                            first_part(b + 1, 1 - s)
                        slot = (s * KW + k) % 2
                        act.wait_ge(rows_ready, b * KW + k + 1 + 2 * KW)
                        act.wait_ge(stored[k], 16 * b + 16)
                        nc.scalar.copy(rows[k][:, :], row_ps[slot][:, :]).then_inc(rows_copied, 1)

                root(0)
                first_part(0, 0)
                with act.Fori(0, PAIRS - 1) as q:
                    for s in range(2):
                        copy_rows(q * 2 + s, s, True)
                copy_rows(NB - 2, 0, True)
                copy_rows(NB - 1, 1, False)

            @block.gpsimd
            def _(pool):
                with pool.Fori(0, PAIRS) as q:
                    for s in range(2):
                        b = q * 2 + s
                        pool.wait_ge(high_ready, b + 1)
                        pool.wait_ge(rows_ready, (b + 1) * KW)
                        pool.sem_inc(copy_begun, 1)
                        nc.gpsimd.tensor_copy(ht_ac[s][0:D, :], ht_ab[s][0:D, :]).then_inc(high_copied, 1)

            @block.vector
            def _(dve):
                dve.sem_inc(own_added, 1)
                dve.sem_inc(low_ready, 1)

                def linker(at):
                    done = [0]

                    def link(ins):
                        done[0] += 1
                        ins.then_inc(step, 1)
                        dve.wait_ge(step, at + done[0])
                    return link

                def normalise(b, s, at):
                    xb = xs[:, bass.ds(b, 1), :].rearrange("p a (k f) -> p (a k) f", k=KW)
                    link = linker(at)
                    norm_steps(nc, link, xb, mean[:, :], rstd[:, :], xc, sq)
                    dve.sem_inc(var_ready, 1)
                    dve.wait_ge(std_ready, b + 1)
                    link(nc.vector.reciprocal(rstd[:, :], rstd[:, :]))
                    dve.wait_ge(turned, b + 1)
                    link(nc.vector.scalar_tensor_tensor(
                        out=h[s][:, :, :], in0=xc[:, :, :], scalar=0.0,
                        in1=rstd[:, :].unsqueeze(2).to_broadcast([P, KW, D]), op0=ALU.max, op1=ALU.mult))
                    dve.sem_inc(h_ready, 1)

                def split(b, s, at):
                    link = linker(at)
                    dve.wait_ge(high_ready, b + 1)
                    dve.wait_ge(rows_ready, (b + 1) * KW)
                    link(nc.vector.tensor_tensor(rest[D:P, :], ht_ps[0:D, 0:BLK], ht_ab[s][0:D, :],
                                                 ALU.subtract))
                    link(nc.vector.tensor_copy(ht_ab[s][D:P, :], rest[D:P, :]))
                    link(nc.vector.tensor_tensor(ht_ac[s][D:P, :], rest[D:P, :], ht_ab[s][D:P, :],
                                                 ALU.subtract))
                    dve.sem_inc(low_ready, 1)

                def add_own(b):
                    xb = xs[:, bass.ds(b, 1), :].rearrange("p a f -> p (a f)")
                    dve.wait_ge(own_ready, b + 2)
                    nc.vector.tensor_tensor(xb, xb, own_ps[:, 0:KW * D], ALU.add).then_inc(own_added, 1)

                normalise(0, 0, 0)
                split(0, 0, NORM_STEPS)
                normalise(1, 1, STEPS)
                begin = STEPS + NORM_STEPS
                with dve.Fori(0, PAIRS - 1) as q:
                    for s in range(2):
                        b = q * 2 + s
                        split(b + 1, 1 - s, begin + b * STEPS)
                        add_own(b)
                        normalise(b + 2, s, begin + b * STEPS + STEPS - NORM_STEPS)
                split(NB - 1, 1, begin + (NB - 2) * STEPS)
                add_own(NB - 2)
                add_own(NB - 1)

            @block.sync
            def _(sp):
                to = table.rearrange("(b p k r) f -> b k p (r f)", p=P, k=KW, r=RELS)
                for k in range(KW):
                    sp.sem_inc(stored[k], 16)
                with sp.Fori(0, NB) as b:
                    for k in range(KW):
                        sp.wait_ge(rows_copied, b * KW + k + 3)
                        sp.dma_start(to[bass.ds(b, 1), k].rearrange("a p f -> (a p) f"),
                                     rows[k][:, :]).then_inc(stored[k], 16)
                for k in range(KW):
                    sp.wait_ge(stored[k], 16 * NB + 16)


def norm_steps(nc, link, xb, mean, var, xc, sq):
    link(nc.vector.tensor_reduce(mean, xb, AX.X, ALU.add))
    link(nc.vector.tensor_scalar(mean, mean, 1.0 / D, None, ALU.mult))
    link(nc.vector.tensor_tensor(xc[:, :, :], xb, mean.unsqueeze(2).to_broadcast([P, KW, D]), ALU.subtract))
    link(nc.vector.tensor_tensor(sq[:, :, :], xc[:, :, :], xc[:, :, :], ALU.mult))
    link(nc.vector.tensor_reduce(var, sq[:, :, :], AX.X, ALU.add))
    link(nc.vector.tensor_scalar(var, var, 1.0 / D, EPS, ALU.mult, ALU.add))


def layer_phase(nc, sem, layer, env):
    name = f"layer{layer}_"
    mlp = layer == 2
    final = layer == 3
    nxt = layer + 1
    acc = env["hidden_acc"] if mlp else env["acc"]
    table, next_table = env["tables"][layer], env["tables"][nxt]
    idx = env["idx_rel"] if layer == 0 else env["idx_src"]
    own_weights, sum_weights = env["own_weights"][nxt], env["sum_weights"][layer]
    wp3b, w_edge, share = env["wp3b"], env["w_edge"], env["share"]
    ident, ident_bf, iota = env["ident"], env["ident_bf"], env["iota"]
    xs, rel_dst, edge_attr, out = env["xs"], env["rel_dst"], env["edge_attr"], env["out"]
    width = H if mlp else D
    sums = D + FE + 1 if layer == 0 else width

    idx_in = [sem(name + f"idx_in{g}") for g in range(PER)]
    gather_begun = sem(name + "gather_begun")
    branch_begun = sem(name + "branch_begun")
    gathered = [sem(name + f"gathered{g}") for g in range(PER)]
    sel_ready = sem(name + "sel_ready")
    summed = sem(name + "summed")
    acc_added = sem(name + "acc_added")
    cleared = sem(name + "cleared")
    shifted = sem(name + "shifted")
    if layer in (0, 2):
        attr_in = [sem(name + f"attr_in{g}") for g in range(PER)]
    if layer == 0:
        attr_ready = sem(name + "attr_ready")
    if mlp:
        rcv_in = [sem(name + f"rcv_in{g}") for g in range(PER)]
        flipped = sem(name + "flipped")
        flip_ready = sem(name + "flip_ready")
        pre_ready = sem(name + "pre_ready")
        pre_added = sem(name + "pre_added")
        relu_ready = sem(name + "relu_ready")
    SLOT_PER, SLOT, DONE = 1, 1 + PER - SLOTS, 1 + PER
    block_final = sem(name + "block_final")
    staged = sem(name + "staged")
    lin_ready = sem(name + "lin_ready")
    lin_copied = sem(name + "lin_copied")
    post_ready = sem(name + "post_ready")
    x_posted = sem(name + "x_posted")
    step = sem(name + "step")
    var_ready = sem(name + "var_ready")
    std_ready = sem(name + "std_ready")
    h_ready = sem(name + "h_ready")
    turn_begun = sem(name + "turn_begun")
    turned = sem(name + "turned")
    ht_ready = sem(name + "ht_ready")
    own_ready = sem(name + "own_ready")
    rows_ready = sem(name + "rows_ready")
    rows_copied = sem(name + "rows_copied")
    stored = sem(name + "stored")
    zero_ready = sem(name + "zero_ready")
    ht_zeroed = sem(name + "ht_zeroed")

    with ExitStack() as scope:
        def sb(n, shape, dt=F32):
            return scope.enter_context(nc.sbuf_tensor(name + n, shape, dt))

        def ps(n, shape=(P, 512), dt=F32):
            return scope.enter_context(nc.psum_tensor(name + n, list(shape), dt))

        idx_slot = [sb(f"idx{g}", [P, TILES], I32) for g in range(PER)]
        msg = [sb(f"msg{g}", [P, TILES, P if layer == 0 else width]) for g in range(PER)]
        sel = [sb(f"sel{j}", [P, TILES, P]) for j in range(SLOTS)]
        attr = [sb(f"attr{j}", [P, TILES * FE]) for j in range(SLOTS)] if layer in (0, 2) else None
        sum_ps = [ps(f"sum_ps{i}") for i in range(2)]
        window_iota = ps("window_iota")[:, 0:P]
        if mlp:
            sel_bf = [sb(f"sel_bf{j}", [P, TILES, P], BF16) for j in range(SLOTS)]
            sel_t = [sb(f"sel_t{i}", [P, TILES * P]) for i in range(2)]
            attr_t = [sb(f"attr_t{i}", [P, P]) for i in range(2)]
            rcv = [sb(f"rcv{j}", [P, H]) for j in range(SLOTS)]
            flip_ps = ps("flip_ps")
            sel_ps = flip_ps[:, 0:TILES * P // 2].bitcast(BF16)
            attr_ps = flip_ps[:, TILES * P // 2:TILES * P // 2 + P]
            pre_ps = [ps(f"pre_ps{i}") for i in range(2)]
        stage_rows = {0: D, 1: DEG + 1, 2: H, 3: DEG + 1}[layer]
        stage = sb("stage", [P, BLK])
        lin = sb("lin", [P, BLK]) if final else None
        mean = sb("mean", [P, KW])
        rstd = sb("rstd", [P, KW])
        xc = sb("xc", [P, KW, D])
        sq = sb("sq", [P, KW, D])
        h = sb("h", [P, KW, D])
        own_rows = DEG + 1 if nxt == 2 else D + 1
        ht = sb("ht", [own_rows, BLK])
        rows = sb("rows", [P, 2, KW * H]) if nxt == 2 else None
        zero_rows = sb("zero_rows", [P, H]) if nxt == 2 else None
        post_ps = ps("post_ps")
        own_ps = (post_ps if mlp else ps("own_ps")) if not final else None
        ht_ps = ps("ht_ps") if not final else None
        row_ps = [ps(f"row_ps{i}") for i in range(2)] if nxt == 2 else None
        lin_ps = ps("lin_ps", (P, 1024)) if final else None
        out_w = D + 1 if nxt == 2 else D
        stores = 2 if nxt == 2 else 1
        steps = {0: 9, 1: 12, 2: 10, 3: 1}[layer]
        halves = [range(0, 4), range(4, KW)]
        out_blocks = out[0:(NB - 1) * BLK, :].rearrange("(b p k) f -> b p (k f)", p=P, k=KW)

        def load_passes(eng):
            return eng.value_load(env["passes"][0:1, 0:1], min_val=1, max_val=MAX_PASSES)

        def load_bases(engine_type, p, group, count=PER, highest=N - 1):
            _, values = nc.values_load_multi_w_load_instructions(
                env["base_row"][0:1, bass.ds(group, count)], engines=[engine_type], min_val=0, max_val=N - 1)
            return [nc.s_assert_within(v + p * P, min_val=0, max_val=highest,
                                       skip_runtime_bounds_check_because="the table is zero where p is not")
                    for v in values]

        def run(eng, engine_type, edges, nodes, each_pass=None):
            n_passes = load_passes(eng)
            with eng.Fori(0, n_passes) as p:
                with eng.Fori(0, NB) as b:
                    _, (lo, hi) = nc.values_load_multi_w_load_instructions(
                        env["schedule"][0:1, bass.ds(b, 2)], engines=[engine_type], min_val=0, max_val=ITERS)
                    with eng.If(lo < hi):
                        with eng.Fori(lo, hi) as i:
                            edges(p, nc.s_assert_within(
                                i, min_val=0, max_val=ITERS - 1,
                                skip_runtime_bounds_check_because="the schedule ends at ITERS"))
                    with eng.If(p == n_passes - 1):
                        nodes(b)
                if each_pass:
                    each_pass(p)

        with nc.Block() as block:
            @block.gpsimd
            def _(pool):
                of = table[0] if mlp else table

                def gather(n, g, padding=False):
                    pool.wait_ge(idx_in[g], n * 16 + 16)
                    pool.wait_ge(summed, n * PER + g + SLOT_PER)
                    pool.sem_inc(gather_begun, 1)
                    for u in range(1 if padding else TILES):
                        nc.gpsimd.indirect_dma_start(
                            msg[g][:, u, 0:width], None, of,
                            bass.IndirectOffsetOnAxis(ap=idx_slot[g][:, u:u + 1], axis=0),
                        ).then_inc(gathered[g], 16 * TILES if padding else 16)

                with pool.Fori(0, load_passes(pool)) as p:
                    with pool.Fori(0, ITERS - 1) as i:
                        for g in range(PER):
                            gather(p * ITERS + i, g)
                    for g in range(PER):
                        gather(p * ITERS + (ITERS - 1), g, padding=(ITERS * PER - PER + g) * GE >= E)

            @block.sync
            def _(sp):
                full = E // GE
                tail_parts = (E - full * GE) // TILES
                groups = edge_attr[0:full * GE, :].rearrange("(g p u) f -> g p (u f)", p=P, u=TILES)

                def load_idx(i, g):
                    sp.dma_start(idx_slot[g][:, :],
                                 idx[:, bass.ds((i * PER + g) * TILES, TILES)]).then_inc(idx_in[g], 16)

                def load_attr(n, i, g, base):
                    j = g % SLOTS
                    sp.wait_ge(flipped if mlp else attr_ready, n * PER + g + 1)
                    if (ITERS - 1) * PER + g < full:
                        at = nc.s_assert_within(i * PER + g, min_val=0, max_val=full - 1,
                                                skip_runtime_bounds_check_because="i is below ITERS")
                        sp.dma_start(attr[j][:, :],
                                     groups[bass.ds(at, 1)].rearrange("a p f -> (a p) f")
                                     ).then_inc(attr_in[g], 16)
                    else:
                        sp.sem_inc(branch_begun, 1)
                        with sp.If(i < ITERS - 1):
                            safe = nc.s_assert_within(
                                i * PER + g, min_val=0, max_val=full - 1,
                                skip_runtime_bounds_check_because="i is below the last iteration")
                            sp.dma_start(attr[j][:, :],
                                         groups[bass.ds(safe, 1)].rearrange("a p f -> (a p) f")
                                         ).then_inc(attr_in[g], 16)
                        with sp.Else():
                            if (ITERS - 1) * PER + g == full:
                                sp.dma_start(attr[j][0:tail_parts, :],
                                             edge_attr[full * GE:E, :].rearrange("(p u) f -> p (u f)",
                                                                                 u=TILES)
                                             ).then_inc(attr_in[g], 16)
                            else:
                                sp.dma_start(attr[j][:, :], groups[full - 1]).then_inc(attr_in[g], 16)
                    if mlp:
                        sp.wait_ge(pre_ready, n * PER + g + 1)
                        sp.dma_start(rcv[j][:, :],
                                     table[1][bass.ds(base, P), :]).then_inc(rcv_in[g], 16)

                for g in range(PER):
                    load_idx(0, g)
                if attr is not None:
                    bases = load_bases(SP_ENGINE, 0, 0, SLOTS) if mlp else [None] * SLOTS
                    for g in range(SLOTS):
                        load_attr(0, 0, g, bases[g])
                    sp.sem_inc(branch_begun, 1)
                with sp.Fori(0, load_passes(sp)) as p:
                    with sp.Fori(0, ITERS) as i:
                        n = p * ITERS + i
                        bases = load_bases(SP_ENGINE, p, i * PER + SLOTS, highest=NPAD) if mlp else [None] * PER
                        following = sp.snap((i + 1) % ITERS)
                        for g in range(PER):
                            sp.wait_ge(gathered[g], (n + 1) * TILES * 16)
                            load_idx(i + 1, g)
                            if attr is None:
                                continue
                            if g + SLOTS < PER:
                                load_attr(n, i, g + SLOTS, bases[g])
                            else:
                                load_attr(n + 1, following, g + SLOTS - PER, bases[g])
                n_passes = load_passes(sp)
                ahead = idx_in + (attr_in[0:SLOTS] if attr else []) + (rcv_in[0:SLOTS] if mlp else [])
                for loaded in ahead:
                    sp.wait_ge(loaded, n_passes * (ITERS * 16) + 16)
                sp.sem_inc(branch_begun, 1)

            @block.scalar
            def _(act):
                if mlp:
                    act.sem_inc(flip_ready, 1)
                act.sem_inc(stored, 16 * stores)
                if layer == 0:
                    act.sem_inc(attr_ready, SLOTS)
                    for g in range(PER):
                        nc.scalar.activation(msg[g][:, :, D + FE:D + FE + 1],
                                             ident[:, 0:TILES].unsqueeze(2), ACT.Copy, bias=1.0, scale=0.0)
                if not final:
                    act.sem_inc(ht_ready, 1)
                if nxt == 2:
                    act.sem_inc(rows_copied, 2)

                def place_attr(n, g):
                    j = g % SLOTS
                    act.wait_ge(attr_in[g], n * 16 + 16)
                    act.wait_ge(summed, n * PER + g + SLOT_PER)
                    nc.scalar.copy(msg[g][:, :, D:D + FE],
                                   attr[j][:, :].rearrange("p (u f) -> p u f", u=TILES)).then_inc(attr_ready, 1)

                def copy_flipped(n, g):
                    act.wait_ge(flipped, n * PER + g + 1 + SLOTS)
                    act.wait_ge(pre_ready, n * PER + g + 3)
                    nc.scalar.copy(attr_t[g % 2][:, :], attr_ps)
                    nc.scalar.copy(sel_t[g % 2][:, :], sel_ps).then_inc(flip_ready, 1)

                def widen(g):
                    j = g % SLOTS
                    nc.scalar.copy(sel[j][:, :, :], sel_bf[j][:, :, :])

                def relu(n, g):
                    act.wait_ge(pre_added, n * PER + g + DONE)
                    nc.scalar.activation(msg[g][:, :, :], msg[g][:, :, :], ACT.Relu).then_inc(relu_ready, 1)

                def edges(p, i):
                    n = p * ITERS + i
                    if layer == 0:
                        for g in range(PER):
                            place_attr(n, g)
                    if mlp:
                        for t in range(PER):
                            copy_flipped(n + (t + 2) // PER, (t + 2) % PER)
                            relu(n, t)
                            widen((t + 2) % PER)

                def nodes(b):
                    act.wait_ge(block_final, b + 1)
                    at = bass.ds(b * BLK, BLK)
                    nc.scalar.copy(stage[0:stage_rows, :], acc[0:stage_rows, at]).then_inc(staged, 1)
                    if final:
                        act.wait_ge(lin_ready, b + 1)
                        half = BLK // 2
                        nc.scalar.copy(lin[:, :].rearrange("p (t c) -> p t c", t=2),
                                       lin_ps[:, :].rearrange("p (t c) -> p t c", t=2)[:, :, 0:half]
                                       ).then_inc(lin_copied, 1)
                        act.wait_ge(x_posted, b + 1)
                        act.sem_inc(branch_begun, 1)
                        with act.If(b < NB - 1):
                            safe = nc.s_assert_within(b, min_val=0, max_val=NB - 2,
                                                      skip_runtime_bounds_check_because="it is tested")
                            act.dma_start(out_blocks[bass.ds(safe, 1)].rearrange("a p f -> (a p) f"),
                                          xs[:, bass.ds(safe, 1), :].rearrange("p a f -> p (a f)")
                                          ).then_inc(stored, 16)
                        return
                    act.wait_ge(var_ready, b + 1)
                    nc.scalar.activation(rstd[:, :], rstd[:, :], ACT.Sqrt).then_inc(std_ready, 1)
                    if nxt != 2:
                        act.wait_ge(h_ready, b + 1)
                        to = next_table.rearrange("(b p k) f -> b p (k f)", p=P, k=KW)
                        act.dma_start(to[bass.ds(b, 1)].rearrange("a p f -> (a p) f"),
                                      h[:, :, :].rearrange("p k f -> p (k f)")).then_inc(stored, 16)
                    for t, windows in enumerate(halves):
                        w0, cols = windows[0] * P, len(windows) * P
                        act.wait_ge(turned, b * 2 + t + 1)
                        nc.scalar.copy(ht[0:D, w0:w0 + cols], ht_ps[0:D, 0:cols]).then_inc(ht_ready, 1)
                    if nxt == 2:
                        act.wait_ge(stored, 16 * stores * (b + 1))
                        for k in range(KW):
                            act.wait_ge(rows_ready, b * KW + k + 1)
                            nc.scalar.copy(rows[:, :, k * H:(k + 1) * H],
                                           row_ps[k % 2][:, 0:2 * H].rearrange("p (t f) -> p t f", t=2)
                                           ).then_inc(rows_copied, 1)
                        act.wait_ge(rows_copied, (b + 1) * KW + 2)
                        for t in range(2):
                            to = next_table[t][0:NPAD, :].rearrange("(b p k) f -> b p (k f)", p=P, k=KW)
                            act.dma_start(to[bass.ds(b, 1)].rearrange("a p f -> (a p) f"),
                                          rows[:, t, :]).then_inc(stored, 16)

                if mlp:
                    copy_flipped(0, 0)
                    copy_flipped(0, 1)
                    widen(0)
                    widen(1)
                run(act, ACT_ENGINE, edges, nodes)
                total = NB * stores + stores
                if final:
                    n0 = (NB - 1) * BLK
                    tail_full = (N - n0) // KW
                    tail_nodes = N - n0 - tail_full * KW
                    act.dma_start(out[n0:n0 + tail_full * KW, :].rearrange("(p k) f -> p (k f)", k=KW),
                                  xs[0:tail_full, NB - 1, :]).then_inc(stored, 16)
                    act.dma_start(out[N - tail_nodes:N, :].rearrange("(a k) f -> a (k f)", a=1),
                                  xs[tail_full:tail_full + 1, NB - 1, 0:tail_nodes * D]).then_inc(stored, 16)
                    total += 1
                if nxt == 2:
                    act.wait_ge(zero_ready, 1)
                    act.dma_start(next_table[1][NPAD:ACC_W, :], zero_rows[:, :]).then_inc(stored, 16)
                    total += 1
                act.wait_ge(stored, 16 * total)

            @block.vector
            def _(dve):
                nc.vector.tensor_copy(window_iota, iota[:, :]).then_inc(shifted, 1)
                if layer == 0:
                    nc.vector.memset(stage[D:D + 1, :], 1.0)
                if nxt == 2:
                    nc.vector.memset(ht[D:DEG + 1, :], 0.0).then_inc(ht_zeroed, 1)
                    dve.wait_ge(ht_zeroed, 1)
                if not final:
                    nc.vector.memset(ht[D:D + 1, :], 1.0)
                if nxt == 2:
                    nc.vector.memset(zero_rows[:, :], 0.0).then_inc(zero_ready, 1)
                nc.vector.memset(acc[0:sums, :], 0.0).then_inc(cleared, 1)
                dve.sem_inc(acc_added, 2)
                if mlp:
                    dve.sem_inc(pre_added, PER)
                dve.wait_ge(shifted, 1)
                dve.wait_ge(cleared, 1)

                def select(n, i, g):
                    j = g % SLOTS
                    dve.wait_ge(summed, n * PER + g + SLOT)
                    rel = rel_dst[:, bass.ds((i * PER + g) * TILES, TILES)]
                    to = sel_bf[j] if mlp else sel[j]
                    nc.vector.tensor_tensor(to[:, :, :], rel.unsqueeze(2).to_broadcast([P, TILES, P]),
                                            window_iota.unsqueeze(1).to_broadcast([P, TILES, P]),
                                            ALU.is_equal).then_inc(sel_ready, 1)

                def add_sender(n, g):
                    dve.wait_ge(pre_ready, n * PER + g + 1 + SLOTS)
                    dve.wait_ge(gathered[g], (n + 1) * TILES * 16)
                    rows_of = msg[g][:, :, :].rearrange("p u f -> p (u f)")
                    nc.vector.tensor_tensor(rows_of, pre_ps[g % 2][:, :], rows_of, ALU.add).then_inc(pre_added, 1)

                def add_sums(n, g, base):
                    dve.wait_ge(summed, n * PER + g + DONE)
                    dve.wait_ge(acc_added, n * PER + g + 2)
                    to = acc[0:sums, bass.ds(base, P)]
                    nc.vector.tensor_tensor(to, to, sum_ps[g % 2][0:sums, 0:P], ALU.add).then_inc(acc_added, 1)

                def edges(p, i):
                    n = p * ITERS + i
                    if mlp:
                        for t in range(PER):
                            add_sender(n, t)
                            select(n + (t + 3) // PER, i + (t + 3) // PER, (t + 3) % PER)
                            if t == 0:
                                bases = load_bases(DVE_ENGINE, p, i * PER)
                            else:
                                add_sums(n, t - 1, bases[t - 1])
                        add_sums(n, PER - 1, bases[PER - 1])
                    else:
                        select(n, i, 0)
                        bases = load_bases(DVE_ENGINE, p, i * PER)
                        for t in range(PER):
                            if t + 1 < PER:
                                select(n, i, t + 1)
                            add_sums(n, t, bases[t])
                    dve.wait_ge(acc_added, (n + 1) * PER + 2)

                def nodes(b):
                    dve.sem_inc(block_final, 1)
                    xb = xs[:, bass.ds(b, 1), :].rearrange("p a (k f) -> p (a k) f", k=KW)
                    done = [0]

                    def link(ins):
                        done[0] += 1
                        ins.then_inc(step, 1)
                        dve.wait_ge(step, b * steps + done[0])

                    if nxt == 2:
                        dve.wait_ge(rows_copied, b * KW + 2)
                        link(nc.vector.tensor_scalar(
                            ht[DEG:DEG + 1, :].rearrange("a (k p) -> a k p", k=KW),
                            acc[DEG:DEG + 1, bass.ds(b * BLK, BLK)].rearrange("a (p k) -> a k p", k=KW),
                            1.0, None, ALU.min))
                    dve.wait_ge(post_ready, b + 1)
                    add = post_ps[:, 0:KW * out_w].rearrange("p (k f) -> p k f", f=out_w)
                    share_b = share[:, bass.ds(b, 1), :].rearrange("p a k -> p (a k)").unsqueeze(2)
                    if nxt == 2:
                        link(nc.vector.tensor_scalar(share_b, add[:, :, D:D + 1], 1.0, None, ALU.max))
                        dve.sem_inc(branch_begun, 1)
                        link(nc.vector.reciprocal(share_b, share_b))
                    if mlp:
                        link(nc.vector.tensor_tensor(sq[:, :, :], add, share_b.to_broadcast([P, KW, D]),
                                                     ALU.mult))
                        add = sq[:, :, :]
                    link(nc.vector.tensor_tensor(xb, xb, add[:, :, 0:D], ALU.add))
                    dve.sem_inc(x_posted, 1)
                    if final:
                        return
                    norm_steps(nc, link, xb, mean[:, :], rstd[:, :], xc, sq)
                    dve.sem_inc(var_ready, 1)
                    dve.wait_ge(std_ready, b + 1)
                    link(nc.vector.reciprocal(rstd[:, :], rstd[:, :]))
                    if nxt != 2:
                        dve.wait_ge(stored, 16 * (b + 1))
                    nc.vector.scalar_tensor_tensor(
                        out=h[:, :, :], in0=xc[:, :, :], scalar=0.0,
                        in1=rstd[:, :].unsqueeze(2).to_broadcast([P, KW, D]), op0=ALU.max,
                        op1=ALU.mult).then_inc(h_ready, 1)
                    dve.wait_ge(own_ready, b + 1)
                    link(nc.vector.tensor_tensor(xb, xb, own_ps[:, 0:KW * D].rearrange(
                        "p (k f) -> p k f", k=KW), ALU.add))
                    dve.sem_inc(branch_begun, 1)

                def next_window(p):
                    nc.vector.tensor_scalar(window_iota, window_iota, float(P), None,
                                            ALU.add).then_inc(shifted, 1)
                    dve.wait_ge(shifted, p + 2)

                if mlp:
                    for g in range(3):
                        select(0, 0, g)
                run(dve, DVE_ENGINE, edges, nodes, next_window)

            @block.tensor
            def _(pe):
                pe.sem_inc(summed, PER)
                if mlp:
                    pe.sem_inc(flipped, SLOTS)
                    pe.sem_inc(pre_ready, SLOTS)

                def flip(n, g):
                    j = g % SLOTS
                    pe.wait_ge(sel_ready, n * PER + g + 1)
                    pe.wait_ge(attr_in[g], n * 16 + 16)
                    pe.wait_ge(flip_ready, n * PER + g + 1)
                    for u in range(TILES):
                        nc.tensor.transpose(sel_ps[:, u * P:(u + 1) * P], sel_bf[j][:, u, :], ident_bf[:, :])
                    nc.tensor.transpose(attr_ps, attr[j][:, :], ident[:, :]).then_inc(flipped, 1)

                def hidden(n, g):
                    j = g % SLOTS
                    pe.wait_ge(flip_ready, n * PER + g + 2)
                    pe.wait_ge(rcv_in[g], n * 16 + 16)
                    pe.wait_ge(pre_added, n * PER + g + DONE - 2)
                    nc.tensor.matmul(pre_ps[g % 2][:, :], attr_t[g % 2][:, :], w_edge[:, :], start=True,
                                     stop=False)
                    for u in range(TILES):
                        last = nc.tensor.matmul(pre_ps[g % 2][:, u * H:(u + 1) * H],
                                                sel_t[g % 2][:, u * P:(u + 1) * P], rcv[j][:, :],
                                                start=False, stop=u == TILES - 1)
                    last.then_inc(pre_ready, 1)

                def sum_up(n, g):
                    j = g % SLOTS
                    pe.wait_ge(acc_added, n * PER + g + 1)
                    if mlp:
                        pe.wait_ge(relu_ready, n * PER + g + 1)
                    else:
                        pe.wait_ge(sel_ready, n * PER + g + 1)
                        pe.wait_ge(gathered[g], (n + 1) * TILES * 16)
                    if layer == 0:
                        pe.wait_ge(attr_ready, n * PER + g + 1 + SLOTS)
                    for u in range(TILES):
                        lhs = msg[g][:, u, 0:sums]
                        last = nc.tensor.matmul(sum_ps[g % 2][0:sums, 0:P], lhs, sel[j][:, u, :], start=u == 0,
                                                stop=u == TILES - 1)
                    last.then_inc(summed, 1)

                def edges(p, i):
                    n = p * ITERS + i
                    for t in range(PER):
                        if mlp:
                            flip(n + (t + 2) // PER, (t + 2) % PER)
                            hidden(n + (t + 1) // PER, (t + 1) % PER)
                        sum_up(n, t)

                def nodes(b):
                    sums_at, weights, k_rows = stage, sum_weights, D + 1 if layer == 0 else stage_rows
                    pe.wait_ge(staged, b + 1)
                    if final:
                        half = BLK // 2
                        for t in range(2):
                            last = nc.tensor.matmul(lin_ps[:, t * 512:t * 512 + half], weights[0:k_rows, :],
                                                    stage[0:k_rows, t * half:(t + 1) * half], start=True,
                                                    stop=True)
                        last.then_inc(lin_ready, 1)
                        pe.wait_ge(lin_copied, b + 1)
                        sums_at, weights, k_rows = lin, wp3b, H
                    for k in range(KW):
                        to, windows = post_ps[:, k * out_w:(k + 1) * out_w], slice(k, BLK, KW)
                        last = nc.tensor.matmul(to, sums_at[0:k_rows, windows], weights[0:k_rows, 0:out_w],
                                                start=True, stop=True)
                    last.then_inc(post_ready, 1)
                    if final:
                        return
                    pe.wait_ge(h_ready, b + 1)
                    for t, windows in enumerate(halves):
                        pe.wait_ge(ht_ready, b * 2 + t + 1)
                        pe.sem_inc(turn_begun, 1)
                        for k in windows:
                            at = (k - windows[0]) * P
                            last = nc.tensor.transpose(ht_ps[0:D, at:at + P], h[:, k, :], ident[:, :])
                        last.then_inc(turned, 1)
                    pe.wait_ge(ht_ready, b * 2 + 3)
                    for k in range(KW):
                        last = nc.tensor.matmul(own_ps[:, k * D:(k + 1) * D], ht[:, k * P:(k + 1) * P],
                                                own_weights[:, 0:D], start=True, stop=True)
                    last.then_inc(own_ready, 1)
                    if nxt != 2:
                        return
                    for k in range(KW):
                        pe.wait_ge(rows_copied, b * KW + k + (2 if k == 0 else 1))
                        nc.tensor.matmul(row_ps[k % 2][:, 0:2 * H],
                                         ht[:, k * P:(k + 1) * P], own_weights[:, D:D + 2 * H],
                                         start=True, stop=True).then_inc(rows_ready, 1)

                if mlp:
                    flip(0, 0)
                    flip(0, 1)
                    hidden(0, 0)
                run(pe, PE_ENGINE, edges, nodes)


_INS = ["x", "src", "dst", "edge_attr_32", "edge_type_16", "L0_gnn_weight", "L0_gnn_h_bias",
        "L0_gnn_loop_weight", "L1_gnn_W", "L1_gnn_b", "L2_gnn_W1", "L2_gnn_b1", "L2_gnn_W2", "L2_gnn_b2",
        "L2_gnn_Wn", "L2_gnn_bn", "L3_gnn_W1", "L3_gnn_b1", "L3_gnn_W2", "L3_gnn_b2"]


def kernel(**inputs):
    import numpy as _np
    import concourse.bacc as _bacc
    from concourse import mybir as _mybir
    from concourse.bass_utils import run_bass_kernel_spmd as _run

    nc = _bacc.Bacc("TRN2", target_bir_lowering=False, num_devices=1)
    arrays, args = {}, []
    for name in _INS:
        a = _np.ascontiguousarray(inputs[name])
        arrays[f"in_{name}_dram"] = a
        args.append(nc.dram_tensor(f"in_{name}_dram", a.shape, _mybir.dt.from_np(a.dtype),
                                   kind="ExternalInput").ap())
    out = nc.dram_tensor("out_0_dram", (N, D), _mybir.dt.float32, kind="ExternalOutput").ap()
    gnn_program(nc, *args, out)
    r = _run(nc, [arrays], core_ids=[0])
    return r.results[0]["out_0_dram"]
```
